# Optimizing a Trainium2 kernel written in Bass

```python
import numpy as np
import jax
import jax.numpy as jnp

def _softmax(x, axis=-1):
    return jax.nn.softmax(x, axis=axis)

def _gelu(x):
    return jax.nn.gelu(x, approximate=True)

def _silu(x):
    return jax.nn.silu(x)

def _sigmoid(x):
    return jax.nn.sigmoid(x)

def _layernorm(x, axis=-1, eps=1e-05):
    m = jnp.mean(x, axis=axis, keepdims=True)
    v = jnp.var(x, axis=axis, keepdims=True)
    return (x - m) / jnp.sqrt(v + eps)

def _scatter_add(tgt, idx, src, axis=0):
    return tgt.at[idx].add(src)

def _segment_sum(src, seg, n):
    return jax.ops.segment_sum(src, seg, n)
kernel_name = 'mk_dlrm_tower_d1_rec_r8_7a3891'

def setup_inputs(seed: int=0):
    np.random.seed(seed)
    _w = jnp.asarray

    def _rec_inputs():
        import jax
        import jax.numpy as jnp
        _tk = jax.random.key(seed)
        dense_ctx = jax.random.normal(jax.random.fold_in(_tk, 190), (2048, 16), jnp.float32)
        ids = jnp.stack([jax.random.randint(jax.random.fold_in(_tk, 200 + f), (2048,), 0, v, jnp.int32) for f, v in enumerate([1250, 1000, 125000, 1000, 1000, 1250, 1000, 1000, 12500, 125000, 12500, 12500, 125000, 1250, 1000, 1250, 1250, 1000, 125000, 1000, 12500, 1000, 12500, 125000, 1250, 1250, 125000, 125000, 1250, 1250, 125000, 12500, 1250, 125000, 1250, 12500, 1000, 12500, 12500])], axis=1)
        tbl_0 = 0.05 * jax.random.normal(jax.random.fold_in(_tk, 500 + 0), (1250, 16), jnp.float32)
        tbl_1 = 0.05 * jax.random.normal(jax.random.fold_in(_tk, 500 + 1), (1000, 16), jnp.float32)
        tbl_2 = 0.05 * jax.random.normal(jax.random.fold_in(_tk, 500 + 2), (125000, 16), jnp.float32)
        tbl_3 = 0.05 * jax.random.normal(jax.random.fold_in(_tk, 500 + 3), (1000, 16), jnp.float32)
        tbl_4 = 0.05 * jax.random.normal(jax.random.fold_in(_tk, 500 + 4), (1000, 16), jnp.float32)
        tbl_5 = 0.05 * jax.random.normal(jax.random.fold_in(_tk, 500 + 5), (1250, 16), jnp.float32)
        tbl_6 = 0.05 * jax.random.normal(jax.random.fold_in(_tk, 500 + 6), (1000, 16), jnp.float32)
        tbl_7 = 0.05 * jax.random.normal(jax.random.fold_in(_tk, 500 + 7), (1000, 16), jnp.float32)
        tbl_8 = 0.05 * jax.random.normal(jax.random.fold_in(_tk, 500 + 8), (12500, 16), jnp.float32)
        tbl_9 = 0.05 * jax.random.normal(jax.random.fold_in(_tk, 500 + 9), (125000, 16), jnp.float32)
        tbl_10 = 0.05 * jax.random.normal(jax.random.fold_in(_tk, 500 + 10), (12500, 16), jnp.float32)
        tbl_11 = 0.05 * jax.random.normal(jax.random.fold_in(_tk, 500 + 11), (12500, 16), jnp.float32)
        tbl_12 = 0.05 * jax.random.normal(jax.random.fold_in(_tk, 500 + 12), (125000, 16), jnp.float32)
        tbl_13 = 0.05 * jax.random.normal(jax.random.fold_in(_tk, 500 + 13), (1250, 16), jnp.float32)
        tbl_14 = 0.05 * jax.random.normal(jax.random.fold_in(_tk, 500 + 14), (1000, 16), jnp.float32)
        tbl_15 = 0.05 * jax.random.normal(jax.random.fold_in(_tk, 500 + 15), (1250, 16), jnp.float32)
        tbl_16 = 0.05 * jax.random.normal(jax.random.fold_in(_tk, 500 + 16), (1250, 16), jnp.float32)
        tbl_17 = 0.05 * jax.random.normal(jax.random.fold_in(_tk, 500 + 17), (1000, 16), jnp.float32)
        tbl_18 = 0.05 * jax.random.normal(jax.random.fold_in(_tk, 500 + 18), (125000, 16), jnp.float32)
        tbl_19 = 0.05 * jax.random.normal(jax.random.fold_in(_tk, 500 + 19), (1000, 16), jnp.float32)
        tbl_20 = 0.05 * jax.random.normal(jax.random.fold_in(_tk, 500 + 20), (12500, 16), jnp.float32)
        tbl_21 = 0.05 * jax.random.normal(jax.random.fold_in(_tk, 500 + 21), (1000, 16), jnp.float32)
        tbl_22 = 0.05 * jax.random.normal(jax.random.fold_in(_tk, 500 + 22), (12500, 16), jnp.float32)
        tbl_23 = 0.05 * jax.random.normal(jax.random.fold_in(_tk, 500 + 23), (125000, 16), jnp.float32)
        tbl_24 = 0.05 * jax.random.normal(jax.random.fold_in(_tk, 500 + 24), (1250, 16), jnp.float32)
        tbl_25 = 0.05 * jax.random.normal(jax.random.fold_in(_tk, 500 + 25), (1250, 16), jnp.float32)
        tbl_26 = 0.05 * jax.random.normal(jax.random.fold_in(_tk, 500 + 26), (125000, 16), jnp.float32)
        tbl_27 = 0.05 * jax.random.normal(jax.random.fold_in(_tk, 500 + 27), (125000, 16), jnp.float32)
        tbl_28 = 0.05 * jax.random.normal(jax.random.fold_in(_tk, 500 + 28), (1250, 16), jnp.float32)
        tbl_29 = 0.05 * jax.random.normal(jax.random.fold_in(_tk, 500 + 29), (1250, 16), jnp.float32)
        tbl_30 = 0.05 * jax.random.normal(jax.random.fold_in(_tk, 500 + 30), (125000, 16), jnp.float32)
        tbl_31 = 0.05 * jax.random.normal(jax.random.fold_in(_tk, 500 + 31), (12500, 16), jnp.float32)
        tbl_32 = 0.05 * jax.random.normal(jax.random.fold_in(_tk, 500 + 32), (1250, 16), jnp.float32)
        tbl_33 = 0.05 * jax.random.normal(jax.random.fold_in(_tk, 500 + 33), (125000, 16), jnp.float32)
        tbl_34 = 0.05 * jax.random.normal(jax.random.fold_in(_tk, 500 + 34), (1250, 16), jnp.float32)
        tbl_35 = 0.05 * jax.random.normal(jax.random.fold_in(_tk, 500 + 35), (12500, 16), jnp.float32)
        tbl_36 = 0.05 * jax.random.normal(jax.random.fold_in(_tk, 500 + 36), (1000, 16), jnp.float32)
        tbl_37 = 0.05 * jax.random.normal(jax.random.fold_in(_tk, 500 + 37), (12500, 16), jnp.float32)
        tbl_38 = 0.05 * jax.random.normal(jax.random.fold_in(_tk, 500 + 38), (12500, 16), jnp.float32)
        _rk = jax.random.fold_in(_tk, 7)
        W_top1 = 0.0606339 * jax.random.normal(jax.random.fold_in(_tk, 801), (272, 512), jnp.float32)
        W_top2 = 0.0441942 * jax.random.normal(jax.random.fold_in(_tk, 802), (512, 256), jnp.float32)
        W_top3 = 0.0625 * jax.random.normal(jax.random.fold_in(_tk, 803), (256, 1), jnp.float32)
        b_top1 = jnp.zeros((512,), jnp.float32)
        b_top2 = jnp.zeros((256,), jnp.float32)
        return (dense_ctx, ids, tbl_0, tbl_1, tbl_2, tbl_3, tbl_4, tbl_5, tbl_6, tbl_7, tbl_8, tbl_9, tbl_10, tbl_11, tbl_12, tbl_13, tbl_14, tbl_15, tbl_16, tbl_17, tbl_18, tbl_19, tbl_20, tbl_21, tbl_22, tbl_23, tbl_24, tbl_25, tbl_26, tbl_27, tbl_28, tbl_29, tbl_30, tbl_31, tbl_32, tbl_33, tbl_34, tbl_35, tbl_36, tbl_37, tbl_38, W_top1, b_top1, W_top2, b_top2, W_top3)
    dense_ctx, ids, tbl_0, tbl_1, tbl_2, tbl_3, tbl_4, tbl_5, tbl_6, tbl_7, tbl_8, tbl_9, tbl_10, tbl_11, tbl_12, tbl_13, tbl_14, tbl_15, tbl_16, tbl_17, tbl_18, tbl_19, tbl_20, tbl_21, tbl_22, tbl_23, tbl_24, tbl_25, tbl_26, tbl_27, tbl_28, tbl_29, tbl_30, tbl_31, tbl_32, tbl_33, tbl_34, tbl_35, tbl_36, tbl_37, tbl_38, W_top1, b_top1, W_top2, b_top2, W_top3 = _rec_inputs()

    def _L0_rec_setup():
        import jax, jax.numpy as jnp
        import numpy as np
        B, F0, D = (256, 39, 16)
        LAYER_SIZES = [128, 128, 128]
        key = jax.random.key(seed)
        ks = jax.random.split(key, 1 + 2 * len(LAYER_SIZES))
        inputs = jax.random.normal(ks[0], (B, F0, D), dtype=jnp.float32)
        out = {'inputs': inputs}
        field_nums = [F0]
        for i, size in enumerate(LAYER_SIZES):
            fk = field_nums[-1]
            fan_in = F0 * fk
            scale = np.sqrt(2.0 / (fan_in + size)).astype(np.float32)
            out[f'w{i}'] = jax.random.normal(ks[1 + 2 * i], (F0, fk, size), dtype=jnp.float32) * scale
            out[f'b{i}'] = jnp.zeros((size,), dtype=jnp.float32)
            field_nums.append(size // 2)
        return out
    _L0_rec_all = _L0_rec_setup()
    _L0_rec_in = {k: v for k, v in _L0_rec_all.items() if k in ('w0', 'w1', 'w2', 'b0', 'b1', 'b2')}
    del _L0_rec_all
    return {'dense_ctx': dense_ctx, 'ids': ids, 'tbl_0': tbl_0, 'tbl_1': tbl_1, 'tbl_2': tbl_2, 'tbl_3': tbl_3, 'tbl_4': tbl_4, 'tbl_5': tbl_5, 'tbl_6': tbl_6, 'tbl_7': tbl_7, 'tbl_8': tbl_8, 'tbl_9': tbl_9, 'tbl_10': tbl_10, 'tbl_11': tbl_11, 'tbl_12': tbl_12, 'tbl_13': tbl_13, 'tbl_14': tbl_14, 'tbl_15': tbl_15, 'tbl_16': tbl_16, 'tbl_17': tbl_17, 'tbl_18': tbl_18, 'tbl_19': tbl_19, 'tbl_20': tbl_20, 'tbl_21': tbl_21, 'tbl_22': tbl_22, 'tbl_23': tbl_23, 'tbl_24': tbl_24, 'tbl_25': tbl_25, 'tbl_26': tbl_26, 'tbl_27': tbl_27, 'tbl_28': tbl_28, 'tbl_29': tbl_29, 'tbl_30': tbl_30, 'tbl_31': tbl_31, 'tbl_32': tbl_32, 'tbl_33': tbl_33, 'tbl_34': tbl_34, 'tbl_35': tbl_35, 'tbl_36': tbl_36, 'tbl_37': tbl_37, 'tbl_38': tbl_38, 'W_top1': W_top1, 'b_top1': b_top1, 'W_top2': W_top2, 'b_top2': b_top2, 'W_top3': W_top3, 'L0_rec_w0': _L0_rec_in['w0'], 'L0_rec_w1': _L0_rec_in['w1'], 'L0_rec_w2': _L0_rec_in['w2'], 'L0_rec_b0': _L0_rec_in['b0'], 'L0_rec_b1': _L0_rec_in['b1'], 'L0_rec_b2': _L0_rec_in['b2']}

def reference(dense_ctx, ids, tbl_0, tbl_1, tbl_2, tbl_3, tbl_4, tbl_5, tbl_6, tbl_7, tbl_8, tbl_9, tbl_10, tbl_11, tbl_12, tbl_13, tbl_14, tbl_15, tbl_16, tbl_17, tbl_18, tbl_19, tbl_20, tbl_21, tbl_22, tbl_23, tbl_24, tbl_25, tbl_26, tbl_27, tbl_28, tbl_29, tbl_30, tbl_31, tbl_32, tbl_33, tbl_34, tbl_35, tbl_36, tbl_37, tbl_38, W_top1, b_top1, W_top2, b_top2, W_top3, L0_rec_w0, L0_rec_w1, L0_rec_w2, L0_rec_b0, L0_rec_b1, L0_rec_b2):
    import jax
    import jax.numpy as jnp

    def _L0_rec_ref(inputs, w0, w1, w2, b0, b1, b2):
        import jax, jax.numpy as jnp
        import numpy as np
        B, F0, D = (256, 39, 16)
        LAYER_SIZES = [128, 128, 128]
        x0 = inputs
        xk = inputs
        params = [(w0, b0), (w1, b1), (w2, b2)]
        n_layers = len(params)
        direct = []
        for idx, (W, b) in enumerate(params):
            z = jnp.einsum('bhd,bkd,hks->bsd', x0, xk, W) + b[None, :, None]
            z = jax.nn.relu(z)
            if idx != n_layers - 1:
                half = z.shape[1] // 2
                xk = z[:, :half, :]
                direct.append(z[:, half:, :])
            else:
                direct.append(z)
        logit = jnp.sum(jnp.concatenate(direct, axis=1), axis=-1)
        return logit
    e = jnp.stack([tbl_0[ids[:, 0]], tbl_1[ids[:, 1]], tbl_2[ids[:, 2]], tbl_3[ids[:, 3]], tbl_4[ids[:, 4]], tbl_5[ids[:, 5]], tbl_6[ids[:, 6]], tbl_7[ids[:, 7]], tbl_8[ids[:, 8]], tbl_9[ids[:, 9]], tbl_10[ids[:, 10]], tbl_11[ids[:, 11]], tbl_12[ids[:, 12]], tbl_13[ids[:, 13]], tbl_14[ids[:, 14]], tbl_15[ids[:, 15]], tbl_16[ids[:, 16]], tbl_17[ids[:, 17]], tbl_18[ids[:, 18]], tbl_19[ids[:, 19]], tbl_20[ids[:, 20]], tbl_21[ids[:, 21]], tbl_22[ids[:, 22]], tbl_23[ids[:, 23]], tbl_24[ids[:, 24]], tbl_25[ids[:, 25]], tbl_26[ids[:, 26]], tbl_27[ids[:, 27]], tbl_28[ids[:, 28]], tbl_29[ids[:, 29]], tbl_30[ids[:, 30]], tbl_31[ids[:, 31]], tbl_32[ids[:, 32]], tbl_33[ids[:, 33]], tbl_34[ids[:, 34]], tbl_35[ids[:, 35]], tbl_36[ids[:, 36]], tbl_37[ids[:, 37]], tbl_38[ids[:, 38]]], axis=1)
    z = _L0_rec_ref(e, L0_rec_w0, L0_rec_w1, L0_rec_w2, L0_rec_b0, L0_rec_b1, L0_rec_b2)
    z = z.reshape(z.shape[0], -1)
    h = jnp.concatenate([z, dense_ctx], axis=1)
    h = jnp.maximum(h @ W_top1 + b_top1, 0.0)
    h = jnp.maximum(h @ W_top2 + b_top2, 0.0)
    y = h @ W_top3
    return y

_drawn_inputs = setup_inputs


def setup_inputs(seed=0):
    import zlib

    import numpy as np

    out = dict(_drawn_inputs(seed))
    spreads = {'b_top1': (0.0, 2.0),
     'b_top2': (0.0, 2.0),
     'L0_rec_b0': (0.0, 0.345),
     'L0_rec_b1': (0.0, 0.527),
     'L0_rec_b2': (0.0, 0.8)}
    factors = {'tbl_0': 8.0,
     'tbl_1': 8.0,
     'tbl_2': 8.0,
     'tbl_3': 8.0,
     'tbl_4': 8.0,
     'tbl_5': 8.0,
     'tbl_6': 8.0,
     'tbl_7': 8.0,
     'tbl_8': 8.0,
     'tbl_9': 8.0,
     'tbl_10': 8.0,
     'tbl_11': 8.0,
     'tbl_12': 8.0,
     'tbl_13': 8.0,
     'tbl_14': 8.0,
     'tbl_15': 8.0,
     'tbl_16': 8.0,
     'tbl_17': 8.0,
     'tbl_18': 8.0,
     'tbl_19': 8.0,
     'tbl_20': 8.0,
     'tbl_21': 8.0,
     'tbl_22': 8.0,
     'tbl_23': 8.0,
     'tbl_24': 8.0,
     'tbl_25': 8.0,
     'tbl_26': 8.0,
     'tbl_27': 8.0,
     'tbl_28': 8.0,
     'tbl_29': 8.0,
     'tbl_30': 8.0,
     'tbl_31': 8.0,
     'tbl_32': 8.0,
     'tbl_33': 8.0,
     'tbl_34': 8.0,
     'tbl_35': 8.0,
     'tbl_36': 8.0,
     'tbl_37': 8.0,
     'tbl_38': 8.0,
     'L0_rec_w0': 8.0,
     'L0_rec_w1': 6.186,
     'L0_rec_w2': 4.749,
     'dense_ctx': 8.0}
    for name, (base, spread) in spreads.items():
        noise = np.random.default_rng([zlib.crc32(name.encode()), seed]).standard_normal(out[name].shape)
        drawn = base * np.exp(spread * noise) if base else spread * noise
        out[name] = jnp.asarray(drawn.astype(out[name].dtype))
    for name, factor in factors.items():
        out[name] = (out[name] * factor).astype(out[name].dtype)
    return out
```

```python
from contextlib import ExitStack

import concourse.bass as bass
from concourse import mybir

SAMPLES, FIELDS, DIM = 2048, 39, 16
HALF = 64
SIZE = 128
P = 128
BLOCKS = SAMPLES // P
TILES = 4
D_TILE = DIM // TILES
COLS = D_TILE * P
BLOCK_COLS = TILES * COLS
CHUNKS = (FIELDS * HALF + P - 1) // P
DELTAS = FIELDS // 2 + 1
BANDS = 3
PAIR_CHUNKS = (DELTAS + BANDS - 1) // BANDS
PAIR_ROWS = BANDS * FIELDS
LAST_PAIR_ROWS = (DELTAS - BANDS * (PAIR_CHUNKS - 1)) * FIELDS
WRAPPED = DELTAS - 1 + FIELDS
GROUP = 2
SLOTS = 8
G12 = CHUNKS // GROUP
G0 = (PAIR_CHUNKS + GROUP - 1) // GROUP
TILE_GROUPS = 2 * G12 + G0
TURN_FIELDS = P // DIM
TURN_PARTS = (FIELDS + TURN_FIELDS - 1) // TURN_FIELDS
TURN_LAST = FIELDS * DIM - (TURN_PARTS - 1) * P
TURNS = 2
CONTEXT = 16
HID1, HID2 = 512, 256
STORES = 16 * 4


def build(nc, t):
    fp32, int32 = mybir.dt.float32, mybir.dt.int32
    ALU = mybir.AluOpType
    ACT = mybir.ActivationFunctionType
    AX = mybir.AxisListType

    with ExitStack() as ctx:
        def sb(name, shape, dt=fp32):
            return ctx.enter_context(nc.sbuf_tensor(name, shape, dt))

        def ps(name, shape):
            return ctx.enter_context(nc.psum_tensor(name, shape, fp32))

        def sem(name):
            return ctx.enter_context(nc.semaphore(name))

        x0t_dram = nc.dram_tensor("x0t_scratch", [BLOCKS, WRAPPED, BLOCK_COLS], fp32)

        ids_all = sb("ids_all", [P, BLOCKS, FIELDS], int32)
        ids_now = sb("ids_now", [P, FIELDS], int32)
        gathered_x = sb("gathered_x", [P, FIELDS * DIM])
        x0t = sb("x0t", [P, TURN_PARTS, P])
        ident = sb("ident", [P, P])
        x0_pair = sb("x0_pair", [PAIR_ROWS, PAIR_CHUNKS, COLS])
        x0_stack = sb("x0_stack", [PAIR_ROWS, COLS])
        x0_bcast = [sb(f"x0_bcast{b}", [P, CHUNKS, COLS]) for b in range(2)]
        products = sb("products", [P, SLOTS, GROUP, COLS])
        w0_sum = sb("w0_sum", [PAIR_ROWS, PAIR_CHUNKS, SIZE])
        w1 = sb("w1", [P, CHUNKS, SIZE])
        w2 = sb("w2", [P, CHUNKS, SIZE])
        w0_swapped = products[0:PAIR_ROWS, 0, :, :].rearrange("p g n -> p (g n)")[:, 0:PAIR_CHUNKS * SIZE]\
            .rearrange("p (c s) -> p c s", s=SIZE)
        bias = [sb(f"bias{l}", [P, 1]) for l in range(3)]
        direct_10 = sb("direct_10", [P, TILES, COLS])
        direct_2 = sb("direct_2", [P, TILES, COLS])
        logit_10 = sb("logit_10", [P, P])
        logit_2 = sb("logit_2", [P, P])
        context_t = sb("context_t", [CONTEXT, SAMPLES])
        wt1_10 = sb("wt1_10", [P, HID1])
        wt1_2 = sb("wt1_2", [P, HID1])
        wt1_ctx = sb("wt1_ctx", [CONTEXT, HID1])
        wt2 = sb("wt2", [P, HID1 // P, HID2])
        wt3 = sb("wt3", [P, HID2 // P])
        bt1 = sb("bt1", [P, HID1 // P])
        bt2 = sb("bt2", [P, HID2 // P])
        hid1 = sb("hid1", [P, HID1 // P, P])
        hid2 = sb("hid2", [P, HID2 // P, P])
        y_row = sb("y_row", [1, P])

        z = [ps(f"z{l}", [P, COLS]) for l in range(3)]
        xk = [None, ps("xk1", [P, COLS]), ps("xk2", [P, COLS])]
        turn = ps("turn", [P, COLS])
        mlp = ps("mlp", [P, COLS])

        cin_w_loaded = sem("cin_w_loaded")
        w0_summed = sem("w0_summed")
        w0_diag_loaded = sem("w0_diag_loaded")
        bias_loaded = sem("bias_loaded")
        mlp_w_loaded = sem("mlp_w_loaded")
        ids_loaded = sem("ids_loaded")
        ident_loaded = sem("ident_loaded")
        ids_copied = sem("ids_copied")
        ids_current = sem("ids_current")
        gathered = sem("gathered")
        turned = sem("turned")
        turn_evac = sem("turn_evac")
        x0t_stored = sem("x0t_stored")
        pair_loaded = sem("pair_loaded")
        bcast_loaded = [sem("bcast_loaded0"), sem("bcast_loaded1")]
        product_ready = sem("product_ready")
        product_used = sem("product_used")
        z_evac = [sem(f"z{l}_evac") for l in range(3)]
        xk_ready = [None, sem("xk1_ready"), sem("xk2_ready")]
        summed_0 = sem("summed_0")
        summed_12 = sem("summed_12")
        h1_ready, h1_evac = sem("h1_ready"), sem("h1_evac")
        h2_ready, h2_evac = sem("h2_ready"), sem("h2_evac")
        y_ready, y_evac = sem("y_ready"), sem("y_evac")
        y_stored = sem("y_stored")

        def first_group(i, q, layer, last=False):
            before = G0 + q * TILE_GROUPS + {1: 0, 0: G12, 2: G12 + G0}[layer]
            if last and q == TILES - 1 and layer == 2:
                before -= G0
            return i * (TILES * TILE_GROUPS) + before

        def groups(layer):
            chunks, last_rows = (PAIR_CHUNKS, LAST_PAIR_ROWS) if layer == 0 else (CHUNKS, HALF)
            return [(c, min(GROUP, chunks - c)) for c in range(0, chunks, GROUP)]

        def rows(layer, c):
            if layer == 0:
                return LAST_PAIR_ROWS if c == PAIR_CHUNKS - 1 else PAIR_ROWS
            return HALF if c == CHUNKS - 1 else P

        block = ctx.enter_context(nc.Block())

        @block.sync
        def _(sp):
            sp.dma_start(ids_all[:], t["ids"].rearrange("(i p) f -> p i f", p=P)).then_inc(ids_loaded, 16)
            sp.dma_start(ident[:], t["ident"]).then_inc(ident_loaded, 16)

            def store_x0t(i, pairs_used=None):
                sp.wait_ge(turn_evac, TURNS * (i + 1))
                rows = x0t_dram[i, :, :].rearrange("f (d b) -> (f d) b", b=P)
                whole = (TURN_PARTS - 1) * P
                again = (WRAPPED - FIELDS) * DIM
                parts = again // P
                for to, n, at in ((0, whole, 0), (whole, TURN_LAST, TURN_PARTS - 1),
                                  (whole + TURN_LAST, parts * P, 0),
                                  (whole + TURN_LAST + parts * P, again - parts * P, parts)):
                    if pairs_used is not None and n < P and at < TURN_PARTS - 1:
                        sp.wait_ge(product_ready, pairs_used)
                    if n >= P:
                        to_dram = rows[to:to + n, :].rearrange("(g p) b -> p g b", p=P)
                        sp.dma_start(to_dram, x0t[:, at:at + n // P, :]).then_inc(x0t_stored, 16)
                    else:
                        sp.dma_start(rows[to:to + n, :], x0t[0:n, at, :]).then_inc(x0t_stored, 16)
                sp.wait_ge(x0t_stored, STORES * (i + 1))

            def source(i, row, q, dims):
                at = x0t_dram[i, row, q * COLS:(q + 1) * COLS]
                return bass.AP(at.tensor, at.offset, dims + [[1, COLS]])

            def load_pair(i, q):
                for r in range(BANDS):
                    chunks = len(range(r, DELTAS, BANDS))
                    sp.dma_start(x0_pair[r * FIELDS:(r + 1) * FIELDS, 0:chunks, :],
                                 source(i, r, q, [[BLOCK_COLS, FIELDS], [BANDS * BLOCK_COLS, chunks]]))\
                        .then_inc(pair_loaded, 16)
                    sp.dma_start(x0_stack[r * FIELDS:(r + 1) * FIELDS, :],
                                 source(i, 0, q, [[BLOCK_COLS, FIELDS]])).then_inc(pair_loaded, 16)

            def load_bcast(i, q):
                for j in range(2):
                    chunks = len(range(j, FIELDS, 2))
                    sp.dma_start(x0_bcast[q % 2][j * HALF:(j + 1) * HALF, 0:chunks, :],
                                 source(i, j, q, [[0, HALF], [2 * BLOCK_COLS, chunks]]))\
                        .then_inc(bcast_loaded[q % 2], 16)

            store_x0t(0)
            load_pair(0, 0)
            load_bcast(0, 0)
            sp.wait_ge(product_ready, G0)
            load_pair(0, 1)
            load_bcast(0, 1)

            def loads(i, last=False):
                for q in range(TILES):
                    if last and q >= TILES - 2:
                        break
                    ahead = (i, q + 2) if q < 2 else (i + 1, q - 2)
                    if q == 2:
                        store_x0t(i + 1, first_group(i, q, 2))
                    else:
                        sp.wait_ge(product_ready, first_group(i, q, 2))
                    load_pair(*ahead)
                    sp.wait_ge(product_ready, first_group(i, q, 2) + G12)
                    load_bcast(*ahead)

            with sp.Fori(0, BLOCKS - 1) as i:
                loads(i)
            loads(BLOCKS - 1, last=True)

        @block.gpsimd
        def _(pool):
            tables = t["tables"]

            def gather(i):
                nc.gpsimd.tensor_copy(ids_now[:], ids_all[:, i, :]).then_inc(ids_copied, 1)
                pool.wait_ge(ids_copied, i + 1)
                pool.sem_inc(ids_current, 1)
                for f in range(FIELDS):
                    pool.indirect_dma_start(
                        gathered_x[:, f * DIM:(f + 1) * DIM], None, tables[f][:, :],
                        bass.IndirectOffsetOnAxis(ids_now[:, f:f + 1], 0)).then_inc(gathered, 16)

            pool.wait_ge(ids_loaded, 16)
            gather(0)
            with pool.Fori(1, BLOCKS) as i:
                pool.wait_ge(gathered, 16 * FIELDS * i)
                pool.wait_ge(turned, TURNS * i)
                gather(i)

        @block.scalar
        def _(act):
            for r in range(BANDS):
                chunks = len(range(r, DELTAS, BANDS))
                part = slice(r * FIELDS, (r + 1) * FIELDS)
                act.dma_start(w0_sum[part, 0:chunks, :],
                              bass.AP(t["w0_k_wrapped"].tensor, r * SIZE,
                                      [[(2 * FIELDS + 1) * SIZE, FIELDS], [BANDS * SIZE, chunks], [1, SIZE]]))\
                    .then_inc(cin_w_loaded, 16)
                act.dma_start(w0_swapped[part, 0:chunks, :],
                              bass.AP(t["w0_h_wrapped"].tensor, r * FIELDS * SIZE,
                                      [[(FIELDS + 1) * SIZE, FIELDS], [BANDS * FIELDS * SIZE, chunks], [1, SIZE]]))\
                    .then_inc(cin_w_loaded, 16)
            whole = (CHUNKS - 1) * P
            for w, name in ((w1, "w1"), (w2, "w2")):
                act.dma_start(w[:, 0:CHUNKS - 1, :], t[name][0:whole, :].rearrange("(c p) s -> p c s", p=P))\
                    .then_inc(cin_w_loaded, 16)
                act.dma_start(w[0:HALF, CHUNKS - 1, :], t[name][whole:, :]).then_inc(cin_w_loaded, 16)
            for l in range(3):
                act.dma_start(bias[l][:], t[f"b{l}"].rearrange("(p a) -> p a", a=1)).then_inc(bias_loaded, 16)
            act.dma_start(wt1_10[HALF:P, :], t["W_top1"][0:HALF, :]).then_inc(mlp_w_loaded, 16)
            act.dma_start(wt1_10[0:HALF, :], t["W_top1"][HALF:P, :]).then_inc(mlp_w_loaded, 16)
            act.dma_start(wt1_2[:], t["W_top1"][P:2 * P, :]).then_inc(mlp_w_loaded, 16)
            act.dma_start(wt1_ctx[:], t["W_top1"][2 * P:, :]).then_inc(mlp_w_loaded, 16)
            act.dma_start(wt2[:], t["W_top2"].rearrange("(c p) n -> p c n", p=P)).then_inc(mlp_w_loaded, 16)
            with nc.allow_non_contiguous_dma("a few hundred biases and weights, once"):
                act.dma_start(wt3[:], t["W_top3"].rearrange("(c p) a -> p (c a)", p=P)).then_inc(mlp_w_loaded, 16)
                act.dma_start(bt1[:], t["b_top1"].rearrange("(c p) -> p c", p=P)).then_inc(mlp_w_loaded, 16)
                act.dma_start(bt2[:], t["b_top2"].rearrange("(c p) -> p c", p=P)).then_inc(mlp_w_loaded, 16)
            act.dma_start(context_t[:], t["context_t"]).then_inc(mlp_w_loaded, 16)
            act.wait_ge(w0_summed, 1)
            act.dma_start(w0_sum[0:FIELDS, 0, :],
                          bass.AP(t["w0_h_wrapped"].tensor, 0, [[(FIELDS + 1) * SIZE, FIELDS], [1, SIZE]]))\
                .then_inc(w0_diag_loaded, 16)

            def evac_turn(i, q):
                act.wait_ge(turned, TURNS * i + q + 1)
                if q == 0 and not (isinstance(i, int) and i == 0):
                    act.wait_ge(x0t_stored, STORES * i)
                if q == 0:
                    nc.scalar.copy(x0t[:, 0:TURN_PARTS - 1, :], turn[:, :].rearrange("p (g b) -> p g b", b=P))\
                        .then_inc(turn_evac, 1)
                else:
                    nc.scalar.copy(x0t[0:TURN_LAST, TURN_PARTS - 1, :], turn[0:TURN_LAST, 0:P])\
                        .then_inc(turn_evac, 1)

            def feed(layer, contracted):
                act.wait_ge(product_used, contracted)
                for to in range(2):
                    last = nc.scalar.activation(xk[layer + 1][to * HALF:(to + 1) * HALF, :], z[layer][0:HALF, :],
                                                ACT.Relu, bias=bias[layer][0:HALF, :])
                last.then_inc(xk_ready[layer + 1], 1)

            def direct_0(i, q):
                if q == 0 and not (isinstance(i, int) and i == 0):
                    act.wait_ge(summed_0, i)
                nc.scalar.activation(direct_10[HALF:P, q, :], z[0][HALF:P, :], ACT.Relu,
                                     bias=bias[0][HALF:P, :]).then_inc(z_evac[0], 1)

            def direct_1(i, q):
                if q == 0 and not (isinstance(i, int) and i == 0):
                    act.wait_ge(summed_12, i)
                nc.scalar.activation(direct_10[0:HALF, q, :], z[1][HALF:P, :], ACT.Relu,
                                     bias=bias[1][HALF:P, :]).then_inc(z_evac[1], 1)

            def direct_all(q, contracted):
                act.wait_ge(product_used, contracted)
                nc.scalar.activation(direct_2[:, q, :], z[2][:, :], ACT.Relu, bias=bias[2][:])\
                    .then_inc(z_evac[2], 1)

            def evac_h1(i):
                act.wait_ge(h1_ready, i + 1)
                for m in range(HID1 // P):
                    last = nc.scalar.activation(hid1[:, m, :], mlp[:, m * P:(m + 1) * P], ACT.Relu,
                                                bias=bt1[:, m:m + 1])
                last.then_inc(h1_evac, 1)

            def evac_h2(i):
                act.wait_ge(h2_ready, i + 1)
                for m in range(HID2 // P):
                    last = nc.scalar.activation(hid2[:, m, :], mlp[:, m * P:(m + 1) * P], ACT.Relu,
                                                bias=bt2[:, m:m + 1])
                last.then_inc(h2_evac, 1)

            def evac_y(i):
                act.wait_ge(y_ready, i + 1)
                if not (isinstance(i, int) and i == 0):
                    act.wait_ge(y_stored, 16 * i)
                nc.scalar.copy(y_row[:], mlp[0:1, 0:P]).then_inc(y_evac, 1)
                act.wait_ge(y_evac, i + 1)
                act.dma_start(t["y"][i, :, :], y_row[:]).then_inc(y_stored, 16)

            act.wait_ge(bias_loaded, 16 * 3)
            for q in range(TURNS):
                evac_turn(0, q)
            feed(0, G0)
            direct_0(0, 0)

            def evacuate(i, first=False, last=False):
                for q in range(TILES):
                    feed(1, first_group(i, q, 1) + G12)
                    direct_1(i, q)
                    if q == 1 and not first:
                        evac_h2(i - 1)
                    if q == 2 and not first:
                        evac_y(i - 1)
                    if q < TILES - 1 or not last:
                        feed(0, first_group(i, q, 0) + G0)
                        direct_0(*((i, q + 1) if q < TILES - 1 else (i + 1, 0)))
                    if q == 0 and not first:
                        evac_h1(i - 1)
                    if q == 1 and not last:
                        evac_turn(i + 1, 0)
                    direct_all(q, first_group(i, q, 2, last) + G12)
                    if q == 1 and not last:
                        evac_turn(i + 1, 1)

            act.wait_ge(mlp_w_loaded, 16 * 9)
            evacuate(0, first=True)
            with act.Fori(1, BLOCKS - 1) as i:
                evacuate(i)
            evacuate(BLOCKS - 1, last=True)
            evac_h1(BLOCKS - 1)
            evac_h2(BLOCKS - 1)
            evac_y(BLOCKS - 1)
            act.wait_ge(y_stored, 16 * BLOCKS)

        @block.vector
        def _(dve):
            dve.wait_ge(cin_w_loaded, 16 * (2 * BANDS + 4))
            nc.vector.tensor_add(w0_sum[:, 0:PAIR_CHUNKS - 1, :], w0_sum[:, 0:PAIR_CHUNKS - 1, :],
                                 w0_swapped[:, 0:PAIR_CHUNKS - 1, :])
            nc.vector.tensor_add(w0_sum[0:LAST_PAIR_ROWS, PAIR_CHUNKS - 1, :],
                                 w0_sum[0:LAST_PAIR_ROWS, PAIR_CHUNKS - 1, :],
                                 w0_swapped[0:LAST_PAIR_ROWS, PAIR_CHUNKS - 1, :]).then_inc(w0_summed, 1)
            dve.wait_ge(w0_summed, 1)

            def multiply(layer, first, ring_free_from=None):
                for g, (c, n) in enumerate(groups(layer)):
                    slot = (first_slot[0] + g) % SLOTS
                    if not isinstance(first, int) or first + g >= SLOTS:
                        dve.wait_ge(product_used, first + g - SLOTS + 1)
                    for part in ([n] if rows(layer, c) == rows(layer, c + n - 1) else [1, 1]):
                        r = rows(layer, c)
                        out = products[0:r, slot, c % GROUP:c % GROUP + part, :]
                        if layer == 0:
                            a = x0_stack[0:r, :]
                            b = x0_pair[0:r, c:c + part, :]
                        else:
                            a = xk[layer][0:r, :]
                            b = bcast_now[0][0:r, c:c + part, :]
                        a = a.unsqueeze(1).broadcast_to([r, part, COLS])
                        last = nc.vector.tensor_tensor(out, a, b, ALU.mult)
                        c += part
                    last.then_inc(product_ready, 1)
                first_slot[0] = (first_slot[0] + len(groups(layer))) % SLOTS

            first_slot, bcast_now = [0], [None]

            def sum_over_d(out, src):
                return nc.vector.tensor_reduce(out, src.rearrange("p q (d b) -> p b q d", b=P), AX.XY, ALU.add)

            def sum_0(i):
                dve.wait_ge(z_evac[0], TILES * (i + 1))
                if not (isinstance(i, int) and i == 0):
                    dve.wait_ge(h1_ready, i)
                sum_over_d(logit_10[HALF:P, :], direct_10[HALF:P, :, :]).then_inc(summed_0, 1)

            def sum_12(i):
                dve.wait_ge(z_evac[1], TILES * (i + 1))
                dve.wait_ge(z_evac[2], TILES * (i + 1))
                sum_over_d(logit_10[0:HALF, :], direct_10[0:HALF, :, :])
                sum_over_d(logit_2[:], direct_2[:, :, :]).then_inc(summed_12, 1)

            dve.wait_ge(pair_loaded, 16 * 2 * BANDS)
            multiply(0, 0)

            def make(i, first=False, last=False):
                for q in range(TILES):
                    tile = TILES * i + q
                    bcast_now[0] = x0_bcast[q % 2]
                    dve.wait_ge(bcast_loaded[q % 2], 32 * (2 * i + q // 2 + 1))
                    dve.wait_ge(xk_ready[1], tile + 1)
                    multiply(1, first_group(i, q, 1))
                    if q == 0 and not first:
                        sum_12(i - 1)
                    if q == TILES - 1:
                        sum_0(i)
                    if q < TILES - 1 or not last:
                        dve.wait_ge(pair_loaded, 16 * 2 * BANDS * (tile + 2))
                        multiply(0, first_group(i, q, 0))
                    dve.wait_ge(xk_ready[2], tile + 1)
                    multiply(2, first_group(i, q, 2, last))

            make(0, first=True)
            with dve.Fori(1, BLOCKS - 1) as i:
                make(i)
            make(BLOCKS - 1, last=True)
            sum_12(BLOCKS - 1)

        @block.tensor
        def _(pe):
            weights = [w0_sum, w1, w2]
            first_slot = [0]

            def turn_tile(i, q):
                nth = TURNS * i + q
                if q == 0:
                    pe.wait_ge(gathered, 16 * FIELDS * (i + 1))
                if not (isinstance(nth, int) and nth == 0):
                    pe.wait_ge(turn_evac, nth)
                for g in range(TURN_PARTS - 1) if q == 0 else [TURN_PARTS - 1]:
                    n = TURN_LAST if q else P
                    last = nc.tensor.transpose(turn[0:n, g % 4 * P:(g % 4 + 1) * P],
                                               gathered_x[:, g * P:g * P + n], ident[:])
                last.then_inc(turned, 1)

            def contract(layer, tile, first):
                if not (isinstance(tile, int) and tile == 0):
                    pe.wait_ge(z_evac[layer], tile)
                chunks = PAIR_CHUNKS if layer == 0 else CHUNKS
                for g, (c0, n) in enumerate(groups(layer)):
                    slot = (first_slot[0] + g) % SLOTS
                    pe.wait_ge(product_ready, first + g + 1)
                    for c in range(c0, c0 + n):
                        r = rows(layer, c)
                        last = nc.tensor.matmul(z[layer][:, :], weights[layer][0:r, c, :],
                                                products[0:r, slot, c - c0, :],
                                                start=(c == 0), stop=(c == chunks - 1))
                    last.then_inc(product_used, 1)
                first_slot[0] = (first_slot[0] + len(groups(layer))) % SLOTS

            def dense_1(i):
                pe.wait_ge(summed_0, i + 1)
                pe.wait_ge(summed_12, i + 1)
                if not (isinstance(i, int) and i == 0):
                    pe.wait_ge(y_evac, i)
                parts = [(wt1_10[:, :], logit_10[:, :]), (wt1_2[:, :], logit_2[:, :]),
                         (wt1_ctx[:, :], context_t[:, bass.ds(i * P, P)])]
                for m in range(HID1 // P):
                    for n, (w, x) in enumerate(parts):
                        last = nc.tensor.matmul(mlp[:, m * P:(m + 1) * P], w[:, m * P:(m + 1) * P], x,
                                                start=(n == 0), stop=(n == len(parts) - 1))
                last.then_inc(h1_ready, 1)

            def dense_2(i):
                pe.wait_ge(h1_evac, i + 1)
                for m in range(HID2 // P):
                    for c in range(HID1 // P):
                        last = nc.tensor.matmul(mlp[:, m * P:(m + 1) * P], wt2[:, c, m * P:(m + 1) * P],
                                                hid1[:, c, :], start=(c == 0), stop=(c == HID1 // P - 1))
                last.then_inc(h2_ready, 1)

            def dense_3(i):
                pe.wait_ge(h2_evac, i + 1)
                for c in range(HID2 // P):
                    last = nc.tensor.matmul(mlp[0:1, 0:P], wt3[:, c:c + 1], hid2[:, c, :],
                                            start=(c == 0), stop=(c == HID2 // P - 1))
                last.then_inc(y_ready, 1)

            pe.wait_ge(ident_loaded, 16)
            for q in range(TURNS):
                turn_tile(0, q)
            pe.wait_ge(cin_w_loaded, 16 * (2 * BANDS + 4))
            pe.wait_ge(w0_summed, 1)
            pe.wait_ge(w0_diag_loaded, 16)
            contract(0, 0, 0)
            pe.wait_ge(mlp_w_loaded, 16 * 9)

            def work(i, first=False, last=False):
                for q in range(TILES):
                    tile = TILES * i + q
                    contract(1, tile, first_group(i, q, 1))
                    if q == 1 and not first:
                        dense_2(i - 1)
                    if q == 2 and not first:
                        dense_3(i - 1)
                    if q < TILES - 1 or not last:
                        contract(0, tile + 1, first_group(i, q, 0))
                    if q == 0 and not first:
                        dense_1(i - 1)
                    if q == 1 and not last:
                        turn_tile(i + 1, 0)
                    contract(2, tile, first_group(i, q, 2, last))
                    if q == 1 and not last:
                        turn_tile(i + 1, 1)

            work(0, first=True)
            with pe.Fori(1, BLOCKS - 1) as i:
                work(i)
            work(BLOCKS - 1, last=True)
            dense_1(BLOCKS - 1)
            dense_2(BLOCKS - 1)
            dense_3(BLOCKS - 1)


def kernel(**inputs):
    import numpy as np
    import concourse.bacc as bacc
    from concourse.bass_utils import run_bass_kernel_spmd

    nc = bacc.Bacc("TRN2", target_bir_lowering=False, num_devices=1)
    arrays, t = {}, {}

    def give(name, a):
        a = np.ascontiguousarray(a)
        arrays["in_" + name] = a
        t[name] = nc.dram_tensor("in_" + name, a.shape, mybir.dt.from_np(a.dtype), kind="ExternalInput").ap()
        return t[name]

    give("ids", inputs["ids"])
    give("ident", np.eye(P, dtype=np.float32))
    give("context_t", np.asarray(inputs["dense_ctx"]).T)
    t["tables"] = [give(f"tbl_{f}", inputs[f"tbl_{f}"]) for f in range(FIELDS)]
    w0 = np.asarray(inputs["L0_rec_w0"])
    give("w0_k_wrapped", np.concatenate([w0, w0], axis=1).reshape(-1, SIZE))
    give("w0_h_wrapped", np.concatenate([w0, w0], axis=0).reshape(-1, SIZE))
    for l in (1, 2):
        give(f"w{l}", np.asarray(inputs[f"L0_rec_w{l}"]).reshape(-1, SIZE))
    for l in range(3):
        give(f"b{l}", inputs[f"L0_rec_b{l}"])
    for name in ("W_top1", "b_top1", "W_top2", "b_top2", "W_top3"):
        give(name, inputs[name])
    t["y"] = nc.dram_tensor("out_y", (BLOCKS, 1, P), mybir.dt.float32, kind="ExternalOutput").ap()
    build(nc, t)
    r = run_bass_kernel_spmd(nc, [arrays], core_ids=[0])
    return np.asarray(r.results[0]["out_y"]).reshape(SAMPLES, 1)
```

```python
from contextlib import ExitStack

import concourse.bass as bass
from concourse import mybir

SAMPLES, FIELDS, DIM = 2048, 39, 16
HALF = 64
SIZE = 128
P = 128
BLOCKS = SAMPLES // P
TILES = 4
D_TILE = DIM // TILES
COLS = D_TILE * P
BLOCK_COLS = TILES * COLS
CHUNKS = (FIELDS * HALF + P - 1) // P
DELTAS = FIELDS // 2 + 1
BANDS = 3
PAIR_CHUNKS = (DELTAS + BANDS - 1) // BANDS
PAIR_ROWS = BANDS * FIELDS
LAST_PAIR_ROWS = (DELTAS - BANDS * (PAIR_CHUNKS - 1)) * FIELDS
WRAPPED = DELTAS - 1 + FIELDS
GROUP = 2
SLOTS = 8
PARTS = 6
PIECE = 4
PIECES = CHUNKS // PIECE
TURN_FIELDS = P // DIM
TURN_PARTS = (FIELDS + TURN_FIELDS - 1) // TURN_FIELDS
TURN_LAST = FIELDS * DIM - (TURN_PARTS - 1) * P
TURNS = 2
WHOLE, ON_VECTOR, ON_POOL = "N", "V", "G"
KINDS = {0: "GVNG", 1: "NGVNGNGVGN", 2: "NGVGNGVNGN"}
EVAC_AFTER = 3
CONTEXT = 16
HID1, HID2 = 512, 256
STORES = 16 * 4


def rows(layer, c):
    if layer == 0:
        return LAST_PAIR_ROWS if c == PAIR_CHUNKS - 1 else PAIR_ROWS
    return HALF if c == CHUNKS - 1 else P


class Group:
    def __init__(self, layer, g, number, split, part):
        chunks = PAIR_CHUNKS if layer == 0 else CHUNKS
        self.layer, self.g, self.c = layer, g, g * GROUP
        self.n = min(GROUP, chunks - self.c)
        self.kind = KINDS[layer][g]
        self.number, self.split, self.part = number, split, part
        self.same_rows = rows(layer, self.c) == rows(layer, self.c + self.n - 1)


def stretch(layers):
    out, number, split, part = [], 0, 0, {ON_VECTOR: 0, ON_POOL: 0, WHOLE: 0}
    for layer in layers:
        out.append([])
        for g, kind in enumerate(KINDS[layer]):
            out[-1].append(Group(layer, g, number, split, part[kind]))
            number, split = number + 1, split + (kind != WHOLE)
            part[kind] += 1
    for group in (g for layer in out for g in layer):
        group.all = [g for layer in out for g in layer]
        group.splits = [g for layer in out for g in layer if g.kind != WHOLE]
    return out, number, split, part


START, START_GROUPS, START_SPLITS, START_PARTS = stretch([0])
BLOCK, BLOCK_GROUPS, BLOCK_SPLITS, BLOCK_PARTS = stretch([1, 0, 2] * TILES)
assert BLOCK_GROUPS % SLOTS == 0 and BLOCK_SPLITS % PARTS == 0
LAST, _, _, _ = stretch([1, 0, 2] * (TILES - 1) + [1, 2])


def is_first(i):
    return isinstance(i, int) and i == 0


def number(i, group):
    return group.number if i is None else i * BLOCK_GROUPS + (START_GROUPS + group.number)


def split_number(i, group):
    return group.split if i is None else i * BLOCK_SPLITS + (START_SPLITS + group.split)


def part_number(i, group):
    return group.part if i is None else i * BLOCK_PARTS[group.kind] + (START_PARTS[group.kind] + group.part)


def slot(i, group):
    return (group.number if i is None else START_GROUPS + group.number) % SLOTS


def part_slot(i, group):
    return (group.split if i is None else START_SPLITS + group.split) % PARTS


def slot_before(i, group):
    at = group.number - SLOTS
    if at >= 0:
        return i, group.all[at]
    if i is None:
        return None, None
    if is_first(i):
        return (None, START[0][at]) if -at <= START_GROUPS else (None, None)
    return i - 1, BLOCK[0][0].all[at]


def splits_before(i, group):
    at = group.split - PARTS
    if at >= 0:
        return number(i, group.splits[at])
    if i is None:
        return None
    if is_first(i):
        start = START[0][0].splits
        return number(None, start[at]) if -at <= len(start) else None
    return number(i - 1, BLOCK[0][0].splits[at])


LAYER_GROUPS = {0: START[0], 1: BLOCK[0], 2: BLOCK[2]}


def group_parts(group):
    if group.same_rows:
        return [(group.c, group.n)]
    return [(c, 1) for c in range(group.c, group.c + group.n)]


def layers(i, q, last):
    if last and q == TILES - 1:
        return LAST[-2], [], LAST[-1]
    return BLOCK[3 * q:3 * q + 3]


def build(nc, t):
    fp32, fp32r, int32 = mybir.dt.float32, mybir.dt.float32r, mybir.dt.int32
    ALU = mybir.AluOpType
    ACT = mybir.ActivationFunctionType
    AX = mybir.AxisListType

    with ExitStack() as ctx:
        def sb(name, shape, dt=fp32):
            return ctx.enter_context(nc.sbuf_tensor(name, shape, dt))

        def ps(name, shape):
            return ctx.enter_context(nc.psum_tensor(name, shape, fp32))

        def sem(name):
            return ctx.enter_context(nc.semaphore(name))

        x0t_dram = nc.dram_tensor("x0t_scratch", [BLOCKS, WRAPPED, BLOCK_COLS], fp32)

        ids_all = sb("ids_all", [P, BLOCKS, FIELDS], int32)
        ids_now = sb("ids_now", [P, FIELDS], int32)
        gathered_x = sb("gathered_x", [P, FIELDS * DIM])
        x0t = sb("x0t", [P, TURN_PARTS, P])
        ident = sb("ident", [P, P])
        x0_pair = sb("x0_pair", [PAIR_ROWS, PAIR_CHUNKS, COLS])
        x0_stack = sb("x0_stack", [PAIR_ROWS, COLS])
        x0_bcast = sb("x0_bcast", [P, CHUNKS, COLS])
        products = sb("products", [P, SLOTS, GROUP, COLS])
        product_hi = sb("product_hi", [P, PARTS, GROUP, COLS], fp32r)
        product_lo = sb("product_lo", [P, PARTS, GROUP, COLS], fp32r)

        place, whole_chunks, split_chunks = {}, 0, 0
        for layer in range(3):
            for c in range(PAIR_CHUNKS if layer == 0 else CHUNKS):
                if KINDS[layer][c // GROUP] == WHOLE:
                    place[layer, c] = whole_chunks
                    whole_chunks += 1
                else:
                    place[layer, c] = split_chunks
                    split_chunks += 1
        w_whole = sb("w_whole", [P, whole_chunks, SIZE])
        w_hi = sb("w_hi", [P, split_chunks, SIZE], fp32r)
        w_lo = sb("w_lo", [P, split_chunks, SIZE], fp32r)
        staged = x0_bcast[:, :, :].rearrange("p c n -> p (c n)")[:, 0:(2 * PAIR_CHUNKS + 2 * CHUNKS) * SIZE]\
            .rearrange("p (c s) -> p c s", s=SIZE)
        w0_sum, w0_swapped = staged[0:PAIR_ROWS, 0:PAIR_CHUNKS, :], staged[0:PAIR_ROWS, PAIR_CHUNKS:2 * PAIR_CHUNKS, :]
        w1 = staged[:, 2 * PAIR_CHUNKS:2 * PAIR_CHUNKS + CHUNKS, :]
        w2 = staged[:, 2 * PAIR_CHUNKS + CHUNKS:, :]
        arrived = [w0_sum, w1, w2]
        bias = [sb(f"bias{l}", [P, 1]) for l in range(3)]
        direct_10 = sb("direct_10", [P, 2, COLS])
        direct_2 = sb("direct_2", [P, COLS])
        tile_sums_10 = sb("tile_sums_10", [P, TILES, P])
        tile_sums_2 = sb("tile_sums_2", [P, TILES, P])
        logit_10 = sb("logit_10", [P, P])
        logit_2 = sb("logit_2", [P, P])
        context_now = sb("context_now", [CONTEXT, P])
        wt1_10 = sb("wt1_10", [P, HID1])
        wt1_2 = sb("wt1_2", [P, HID1])
        wt1_ctx = sb("wt1_ctx", [CONTEXT, HID1])
        wt2 = sb("wt2", [P, HID1 // P, HID2])
        wt3 = sb("wt3", [P, HID2 // P])
        bt1 = sb("bt1", [P, HID1 // P])
        bt2 = sb("bt2", [P, HID2 // P])
        hid1 = sb("hid1", [P, HID1 // P, P])
        hid2 = sb("hid2", [P, HID2 // P, P])
        y_row = sb("y_row", [1, P])

        z = [ps(f"z{l}", [P, COLS]) for l in range(3)]
        xk = [None, ps("xk1", [P, COLS]), ps("xk2", [P, COLS])]
        turn = [ps(f"turn{q}", [P, COLS]) for q in range(TURNS)]
        mlp = ps("mlp", [P, COLS])

        cin_w_loaded = sem("cin_w_loaded")
        w0_summed = sem("w0_summed")
        w0_diag_loaded = sem("w0_diag_loaded")
        bias_loaded = sem("bias_loaded")
        mlp_w_loaded = sem("mlp_w_loaded")
        ids_loaded = sem("ids_loaded")
        ident_loaded = sem("ident_loaded")
        ids_copied = sem("ids_copied")
        ids_current = sem("ids_current")
        gathered = sem("gathered")
        turned = sem("turned")
        turn_evac = sem("turn_evac")
        x0t_stored = sem("x0t_stored")
        pair_loaded = sem("pair_loaded")
        bcast_loaded = [sem(f"bcast_loaded{k}") for k in range(PIECES)]
        context_loaded = sem("context_loaded")
        w_hi_made = sem("w_hi_made")
        w_made = sem("w_made")
        hi_ready = sem("hi_ready")
        lo_ready = {ON_VECTOR: sem("lo_ready_vector"), ON_POOL: sem("lo_ready_pool")}
        product_ready = sem("product_ready")
        product_used = sem("product_used")
        z_evac = [sem(f"z{l}_evac") for l in range(3)]
        xk_ready = [None, sem("xk1_ready"), sem("xk2_ready")]
        summed_10 = sem("summed_10")
        summed_2 = sem("summed_2")
        logits_ready = sem("logits_ready")
        h1_ready, h1_evac = sem("h1_ready"), sem("h1_evac")
        h2_ready, h2_evac = sem("h2_ready"), sem("h2_evac")
        y_ready, y_evac = sem("y_ready"), sem("y_evac")
        y_stored = sem("y_stored")

        block = ctx.enter_context(nc.Block())

        @block.sync
        def _(sp):
            sp.dma_start(ids_all[:], t["ids"].rearrange("(i p) f -> p i f", p=P)).then_inc(ids_loaded, 16)
            sp.dma_start(ident[:], t["ident"]).then_inc(ident_loaded, 16)

            def store_x0t(i, pairs_used=None):
                sp.wait_ge(turn_evac, i + 1)
                rows = x0t_dram[i, :, :].rearrange("f (d b) -> (f d) b", b=P)
                whole = (TURN_PARTS - 1) * P
                again = (WRAPPED - FIELDS) * DIM
                parts = again // P
                for to, n, at in ((0, whole, 0), (whole, TURN_LAST, TURN_PARTS - 1),
                                  (whole + TURN_LAST, parts * P, 0),
                                  (whole + TURN_LAST + parts * P, again - parts * P, parts)):
                    if pairs_used is not None and n < P and at < TURN_PARTS - 1:
                        sp.wait_ge(product_ready, pairs_used)
                    if n >= P:
                        to_dram = rows[to:to + n, :].rearrange("(g p) b -> p g b", p=P)
                        sp.dma_start(to_dram, x0t[:, at:at + n // P, :]).then_inc(x0t_stored, 16)
                    else:
                        sp.dma_start(rows[to:to + n, :], x0t[0:n, at, :]).then_inc(x0t_stored, 16)
                sp.wait_ge(x0t_stored, STORES * (i + 1))

            def source(i, row, q, dims):
                at = x0t_dram[i, row, q * COLS:(q + 1) * COLS]
                return bass.AP(at.tensor, at.offset, dims + [[1, COLS]])

            def load_pair(i, q):
                for r in range(BANDS):
                    chunks = len(range(r, DELTAS, BANDS))
                    sp.dma_start(x0_pair[r * FIELDS:(r + 1) * FIELDS, 0:chunks, :],
                                 source(i, r, q, [[BLOCK_COLS, FIELDS], [BANDS * BLOCK_COLS, chunks]]))\
                        .then_inc(pair_loaded, 16)
                    sp.dma_start(x0_stack[r * FIELDS:(r + 1) * FIELDS, :],
                                 source(i, 0, q, [[BLOCK_COLS, FIELDS]])).then_inc(pair_loaded, 16)

            def load_bcast(i, q, k):
                for j in range(2):
                    chunks = len(range(2 * k * PIECE + j, min(FIELDS, 2 * (k + 1) * PIECE), 2))
                    sp.dma_start(x0_bcast[j * HALF:(j + 1) * HALF, k * PIECE:k * PIECE + chunks, :],
                                 source(i, 2 * k * PIECE + j, q, [[0, HALF], [2 * BLOCK_COLS, chunks]]))\
                        .then_inc(bcast_loaded[k], 16)

            store_x0t(0)
            load_pair(0, 0)
            sp.wait_ge(w_made, 1)
            for k in range(PIECES):
                load_bcast(0, 0, k)
            sp.wait_ge(product_ready, START_GROUPS)
            load_pair(0, 1)

            def loads(i, last=False):
                for q in range(TILES):
                    _, _, second = layers(i, q, last)
                    if q == 2 and not last:
                        store_x0t(i + 1, number(i, second[0]))
                    elif not (last and q >= 2):
                        sp.wait_ge(product_ready, number(i, second[0]))
                    if not (last and q >= 2):
                        load_pair(*((i, q + 2) if q < 2 else (i + 1, q - 2)))
                    if q == 2:
                        if not is_first(i):
                            sp.wait_ge(h1_ready, i)
                        sp.dma_start(context_now[:], t["context_t"][i, :, :]).then_inc(context_loaded, 16)
                    if last and q == TILES - 1:
                        break
                    for k in range(PIECES):
                        sp.wait_ge(product_ready, number(i, second[(k + 1) * PIECE // GROUP - 1]) + 1)
                        load_bcast(*((i, q + 1) if q < TILES - 1 else (i + 1, 0)), k)

            loads(0)
            with sp.Fori(1, BLOCKS - 1) as i:
                loads(i)
            loads(BLOCKS - 1, last=True)

        @block.gpsimd
        def _(pool):
            tables = t["tables"]

            half = (FIELDS + 1) // 2

            def take_ids(i):
                nc.gpsimd.tensor_copy(ids_now[:], ids_all[:, i, :]).then_inc(ids_copied, 1)
                pool.wait_ge(ids_copied, i + 1)
                pool.sem_inc(ids_current, 1)

            def gather(f):
                pool.indirect_dma_start(
                    gathered_x[:, f * DIM:(f + 1) * DIM], None, tables[f][:, :],
                    bass.IndirectOffsetOnAxis(ids_now[:, f:f + 1], 0)).then_inc(gathered, 16)

            def low_part(i, group):
                pool.wait_ge(hi_ready, split_number(i, group) + 1)
                r, at = rows(group.layer, group.c), part_slot(i, group)
                nc.gpsimd.tensor_tensor(product_lo[0:r, at, 0:group.n, :], products[0:r, slot(i, group), 0:group.n, :],
                                        product_hi[0:r, at, 0:group.n, :].bitcast(fp32), ALU.subtract)\
                    .then_inc(lo_ready[ON_POOL], 1)

            pool.wait_ge(ids_loaded, 16)
            take_ids(0)
            for f in range(FIELDS):
                gather(f)
            for group in START[0]:
                if group.kind == ON_POOL:
                    low_part(None, group)
            pool.wait_ge(gathered, 16 * FIELDS)
            pool.wait_ge(turned, TURNS)
            take_ids(1)

            def work(i, next_block, block_after):
                for q in range(TILES):
                    if q == 2 and block_after:
                        pool.wait_ge(gathered, 16 * FIELDS * (i + 2))
                        pool.wait_ge(turned, TURNS * (i + 2))
                        take_ids(i + 2)
                    fields = [] if not (next_block if q < 2 else block_after) else \
                        list(range(0 if is_first(i) else half, FIELDS) if q < 2 else range(half))
                    mine = [g for layer in layers(i, q, not next_block) for g in layer if g.kind == ON_POOL]
                    now = fields[q % 2 * (len(fields) // 2):][:len(fields) // 2] if q % 2 == 0 \
                        else fields[len(fields) // 2:]
                    for n, group in enumerate(mine):
                        low_part(i, group)
                        for f in now[n * len(now) // len(mine):(n + 1) * len(now) // len(mine)]:
                            gather(f)

            work(0, True, True)
            with pool.Fori(1, BLOCKS - 2) as i:
                work(i, True, True)
            work(BLOCKS - 2, True, False)
            work(BLOCKS - 1, False, False)

        @block.scalar
        def _(act):
            for r in range(BANDS):
                chunks = len(range(r, DELTAS, BANDS))
                part = slice(r * FIELDS, (r + 1) * FIELDS)
                act.dma_start(w0_sum[part, 0:chunks, :],
                              bass.AP(t["w0_k_wrapped"].tensor, r * SIZE,
                                      [[(2 * FIELDS + 1) * SIZE, FIELDS], [BANDS * SIZE, chunks], [1, SIZE]]))\
                    .then_inc(cin_w_loaded, 16)
                act.dma_start(w0_swapped[part, 0:chunks, :],
                              bass.AP(t["w0_h_wrapped"].tensor, r * FIELDS * SIZE,
                                      [[(FIELDS + 1) * SIZE, FIELDS], [BANDS * FIELDS * SIZE, chunks], [1, SIZE]]))\
                    .then_inc(cin_w_loaded, 16)
            whole = (CHUNKS - 1) * P
            for w, name in ((w1, "w1"), (w2, "w2")):
                act.dma_start(w[:, 0:CHUNKS - 1, :], t[name][0:whole, :].rearrange("(c p) s -> p c s", p=P))\
                    .then_inc(cin_w_loaded, 16)
                act.dma_start(w[0:HALF, CHUNKS - 1, :], t[name][whole:, :]).then_inc(cin_w_loaded, 16)
            for l in range(3):
                act.dma_start(bias[l][:], t[f"b{l}"].rearrange("(p a) -> p a", a=1)).then_inc(bias_loaded, 16)
            act.dma_start(wt1_10[HALF:P, :], t["W_top1"][0:HALF, :]).then_inc(mlp_w_loaded, 16)
            act.dma_start(wt1_10[0:HALF, :], t["W_top1"][HALF:P, :]).then_inc(mlp_w_loaded, 16)
            act.dma_start(wt1_2[:], t["W_top1"][P:2 * P, :]).then_inc(mlp_w_loaded, 16)
            act.dma_start(wt1_ctx[:], t["W_top1"][2 * P:, :]).then_inc(mlp_w_loaded, 16)
            act.dma_start(wt2[:], t["W_top2"].rearrange("(c p) n -> p c n", p=P)).then_inc(mlp_w_loaded, 16)
            with nc.allow_non_contiguous_dma("a few hundred biases and weights, once"):
                act.dma_start(wt3[:], t["W_top3"].rearrange("(c p) a -> p (c a)", p=P)).then_inc(mlp_w_loaded, 16)
                act.dma_start(bt1[:], t["b_top1"].rearrange("(c p) -> p c", p=P)).then_inc(mlp_w_loaded, 16)
                act.dma_start(bt2[:], t["b_top2"].rearrange("(c p) -> p c", p=P)).then_inc(mlp_w_loaded, 16)
            act.wait_ge(w0_summed, 1)
            act.dma_start(w0_sum[0:FIELDS, 0, :],
                          bass.AP(t["w0_h_wrapped"].tensor, 0, [[(FIELDS + 1) * SIZE, FIELDS], [1, SIZE]]))\
                .then_inc(w0_diag_loaded, 16)

            act.wait_ge(w0_diag_loaded, 16)
            for layer in range(3):
                for group in LAYER_GROUPS[layer]:
                    if group.kind != WHOLE:
                        r, at = rows(layer, group.c), place[layer, group.c]
                        last = nc.scalar.copy(w_hi[0:r, at:at + group.n, :],
                                              arrived[layer][0:r, group.c:group.c + group.n, :])
            last.then_inc(w_hi_made, 1)

            def evac_turns(i):
                act.wait_ge(turned, TURNS * (i + 1))
                if not is_first(i):
                    act.wait_ge(x0t_stored, STORES * i)
                nc.scalar.copy(x0t[:, 0:TURN_PARTS - 1, :], turn[0][:, :].rearrange("p (g b) -> p g b", b=P))
                nc.scalar.copy(x0t[0:TURN_LAST, TURN_PARTS - 1, :], turn[1][0:TURN_LAST, 0:P])\
                    .then_inc(turn_evac, 1)

            def high_part(i, group):
                act.wait_ge(product_ready, number(i, group) + 1)
                before = splits_before(i, group)
                if before is not None:
                    act.wait_ge(product_used, before + 1)
                r, at = rows(group.layer, group.c), part_slot(i, group)
                nc.scalar.copy(product_hi[0:r, at, 0:group.n, :], products[0:r, slot(i, group), 0:group.n, :])\
                    .then_inc(hi_ready, 1)

            def feed(layer, contracted):
                act.wait_ge(product_used, contracted)
                for to in range(2):
                    last = nc.scalar.activation(xk[layer + 1][to * HALF:(to + 1) * HALF, :], z[layer][0:HALF, :],
                                                ACT.Relu, bias=bias[layer][0:HALF, :])
                last.then_inc(xk_ready[layer + 1], 1)

            def direct_0(i, q):
                tile = TILES * i + q
                if not (isinstance(tile, int) and tile < 2):
                    act.wait_ge(summed_10, tile - 1)
                nc.scalar.activation(direct_10[HALF:P, q % 2, :], z[0][HALF:P, :], ACT.Relu,
                                     bias=bias[0][HALF:P, :]).then_inc(z_evac[0], 1)

            def direct_1(i, q):
                nc.scalar.activation(direct_10[0:HALF, q % 2, :], z[1][HALF:P, :], ACT.Relu,
                                     bias=bias[1][HALF:P, :]).then_inc(z_evac[1], 1)

            def direct_all(tile, contracted):
                act.wait_ge(product_used, contracted)
                if not (isinstance(tile, int) and tile == 0):
                    act.wait_ge(summed_2, tile)
                nc.scalar.activation(direct_2[:, :], z[2][:, :], ACT.Relu, bias=bias[2][:])\
                    .then_inc(z_evac[2], 1)

            def evac_h1(i):
                act.wait_ge(h1_ready, i + 1)
                for m in range(HID1 // P):
                    last = nc.scalar.activation(hid1[:, m, :], mlp[:, m * P:(m + 1) * P], ACT.Relu,
                                                bias=bt1[:, m:m + 1])
                last.then_inc(h1_evac, 1)

            def evac_h2(i):
                act.wait_ge(h2_ready, i + 1)
                for m in range(HID2 // P):
                    last = nc.scalar.activation(hid2[:, m, :], mlp[:, m * P:(m + 1) * P], ACT.Relu,
                                                bias=bt2[:, m:m + 1])
                last.then_inc(h2_evac, 1)

            def evac_y(i):
                act.wait_ge(y_ready, i + 1)
                if not is_first(i):
                    act.wait_ge(y_stored, 16 * i)
                nc.scalar.copy(y_row[:], mlp[0:1, 0:P]).then_inc(y_evac, 1)
                act.wait_ge(y_evac, i + 1)
                act.dma_start(t["y"][i, :, :], y_row[:]).then_inc(y_stored, 16)

            act.wait_ge(bias_loaded, 16 * 3)
            evac_turns(0)
            for group in START[0]:
                if group.kind != WHOLE:
                    high_part(None, group)
            feed(0, START_GROUPS)
            direct_0(0, 0)
            act.wait_ge(mlp_w_loaded, 16 * 8)

            def work(i, first=False, last=False):
                for q in range(TILES):
                    first_layer, next_zeroth, second_layer = layers(i, q, last)

                    def read_first():
                        feed(1, number(i, first_layer[-1]) + 1)
                        direct_1(i, q)

                    def before_first():
                        if not (first and q == 0):
                            direct_all(TILES * i + (q - 1), number(i, first_layer[0]))
                        if q == 1 and not first:
                            evac_h1(i - 1)
                        if q == 2 and not first:
                            evac_y(i - 1)
                        if q == 2 and not last:
                            evac_turns(i + 1)

                    def before_second():
                        if next_zeroth:
                            feed(0, number(i, next_zeroth[-1]) + 1)
                            direct_0(*((i, q + 1) if q < TILES - 1 else (i + 1, 0)))
                        if q == 1 and not first:
                            evac_h2(i - 1)

                    for layer, then in ((first_layer, before_first), (next_zeroth, read_first),
                                        (second_layer, before_second)):
                        if not layer:
                            then()
                        for group in layer:
                            if group.kind != WHOLE:
                                high_part(i, group)
                            if group.g == EVAC_AFTER:
                                then()

            work(0, first=True)
            with act.Fori(1, BLOCKS - 1) as i:
                work(i)
            work(BLOCKS - 1, last=True)
            direct_all(TILES * BLOCKS - 1, number(BLOCKS - 1, LAST[-1][-1]) + 1)
            evac_h1(BLOCKS - 1)
            evac_h2(BLOCKS - 1)
            evac_y(BLOCKS - 1)
            act.wait_ge(y_stored, 16 * BLOCKS)

        @block.vector
        def _(dve):
            dve.wait_ge(cin_w_loaded, 16 * (2 * BANDS + 4))
            nc.vector.tensor_add(w0_sum[:, 0:PAIR_CHUNKS - 1, :], w0_sum[:, 0:PAIR_CHUNKS - 1, :],
                                 w0_swapped[:, 0:PAIR_CHUNKS - 1, :])
            nc.vector.tensor_add(w0_sum[0:LAST_PAIR_ROWS, PAIR_CHUNKS - 1, :],
                                 w0_sum[0:LAST_PAIR_ROWS, PAIR_CHUNKS - 1, :],
                                 w0_swapped[0:LAST_PAIR_ROWS, PAIR_CHUNKS - 1, :]).then_inc(w0_summed, 1)
            dve.wait_ge(w0_diag_loaded, 16)
            dve.wait_ge(w_hi_made, 1)
            for layer in range(3):
                for group in LAYER_GROUPS[layer]:
                    for c, n in group_parts(group):
                        r, at, w = rows(layer, c), place[layer, c], arrived[layer]
                        if group.kind == WHOLE:
                            last = nc.vector.tensor_copy(w_whole[0:r, at:at + n, :], w[0:r, c:c + n, :])
                        else:
                            last = nc.vector.tensor_tensor(w_lo[0:r, at:at + n, :], w[0:r, c:c + n, :],
                                                           w_hi[0:r, at:at + n, :].bitcast(fp32), ALU.subtract)
            last.then_inc(w_made, 1)

            def multiply(i, group):
                at, before = slot_before(i, group)
                if before is not None:
                    if before.kind == WHOLE:
                        dve.wait_ge(product_used, number(at, before) + 1)
                    else:
                        dve.wait_ge(lo_ready[before.kind], part_number(at, before) + 1)
                for c, n in group_parts(group):
                    r = rows(group.layer, c)
                    if group.layer == 0:
                        a, b = x0_stack[0:r, :], x0_pair[0:r, c:c + n, :]
                    else:
                        a, b = xk[group.layer][0:r, :], x0_bcast[0:r, c:c + n, :]
                    last = nc.vector.tensor_tensor(products[0:r, slot(i, group), c - group.c:c - group.c + n, :],
                                                   a.unsqueeze(1).broadcast_to([r, n, COLS]), b, ALU.mult)
                last.then_inc(product_ready, 1)

            def low_part(i, group):
                dve.wait_ge(hi_ready, split_number(i, group) + 1)
                r, at = rows(group.layer, group.c), part_slot(i, group)
                nc.vector.tensor_tensor(product_lo[0:r, at, 0:group.n, :], products[0:r, slot(i, group), 0:group.n, :],
                                        product_hi[0:r, at, 0:group.n, :].bitcast(fp32), ALU.subtract)\
                    .then_inc(lo_ready[ON_VECTOR], 1)

            def make(i, layer, tile=None):
                due = []
                for group in layer:
                    if group.layer == 1 and group.c % PIECE == 0:
                        dve.wait_ge(bcast_loaded[group.c // PIECE], 32 * (tile + 1))
                    multiply(i, group)
                    if due and due[0].g + 2 <= group.g:
                        low_part(i, due.pop(0))
                    if group.kind == ON_VECTOR:
                        due.append(group)
                for group in due:
                    low_part(i, group)

            def sum_10(i, q):
                dve.wait_ge(z_evac[0], TILES * i + q + 1)
                dve.wait_ge(z_evac[1], TILES * i + q + 1)
                nc.vector.tensor_reduce(tile_sums_10[:, q, :],
                                        direct_10[:, q % 2, :].rearrange("p (d b) -> p b d", b=P),
                                        AX.X, ALU.add).then_inc(summed_10, 1)

            def sum_2(i, q):
                dve.wait_ge(z_evac[2], TILES * i + q + 1)
                nc.vector.tensor_reduce(tile_sums_2[:, q, :], direct_2[:, :].rearrange("p (d b) -> p b d", b=P),
                                        AX.X, ALU.add).then_inc(summed_2, 1)

            def logits(i):
                dve.wait_ge(summed_10, TILES * (i + 1))
                dve.wait_ge(summed_2, TILES * (i + 1))
                if not is_first(i):
                    dve.wait_ge(h1_ready, i)
                for out, sums in ((logit_10, tile_sums_10), (logit_2, tile_sums_2)):
                    last = nc.vector.tensor_reduce(out[:], sums[:, :, :].rearrange("p q b -> p b q"), AX.X, ALU.add)
                last.then_inc(logits_ready, 1)

            dve.wait_ge(pair_loaded, 16 * 2 * BANDS)
            make(None, START[0])

            def work(i, first=False, last=False):
                for q in range(TILES):
                    tile = TILES * i + q
                    first_layer, next_zeroth, second_layer = layers(i, q, last)
                    dve.wait_ge(xk_ready[1], tile + 1)
                    make(i, first_layer, tile)
                    if q > 0:
                        sum_2(i, q - 1)
                    elif not first:
                        sum_2(i - 1, TILES - 1)
                        logits(i - 1)
                    if next_zeroth:
                        dve.wait_ge(pair_loaded, 16 * 2 * BANDS * (tile + 2))
                        make(i, next_zeroth)
                    dve.wait_ge(xk_ready[2], tile + 1)
                    make(i, second_layer)
                    if q == 0 and not first:
                        dve.wait_ge(logits_ready, i)
                    sum_10(i, q)

            work(0, first=True)
            with dve.Fori(1, BLOCKS - 1) as i:
                work(i)
            work(BLOCKS - 1, last=True)
            sum_2(BLOCKS - 1, TILES - 1)
            logits(BLOCKS - 1)

        @block.tensor
        def _(pe):
            def turn_block(i):
                pe.wait_ge(gathered, 16 * FIELDS * (i + 1))
                if not is_first(i):
                    pe.wait_ge(turn_evac, i)
                for g in range(TURN_PARTS):
                    n = TURN_LAST if g == TURN_PARTS - 1 else P
                    last = nc.tensor.transpose(turn[g // 4][0:n, g % 4 * P:(g % 4 + 1) * P],
                                               gathered_x[:, g * P:g * P + n], ident[:])
                    if g % 4 == 3 or g == TURN_PARTS - 1:
                        last.then_inc(turned, 1)

            def contract(i, layer, tile):
                which = layer[0].layer
                z_now = z[which][:, :]
                if not is_first(tile):
                    pe.wait_ge(z_evac[which], tile)
                for group in layer:
                    chunks = range(group.c, group.c + group.n)
                    ends = group is layer[-1]
                    if group.kind == WHOLE:
                        pe.wait_ge(product_ready, number(i, group) + 1)
                        for c in chunks:
                            r = rows(which, c)
                            last = nc.tensor.matmul(z_now, w_whole[0:r, place[which, c], :],
                                                    products[0:r, slot(i, group), c - group.c, :],
                                                    start=(c == 0), stop=(ends and c == chunks[-1]))
                    else:
                        pe.wait_ge(hi_ready, split_number(i, group) + 1)
                        for c in chunks:
                            r, at = rows(which, c), place[which, c]
                            hi = product_hi[0:r, part_slot(i, group), c - group.c, :]
                            nc.tensor.matmul(z_now, w_hi[0:r, at, :], hi, start=(c == 0), stop=False)
                            nc.tensor.matmul(z_now, w_lo[0:r, at, :], hi, start=False, stop=False)
                        pe.wait_ge(lo_ready[group.kind], part_number(i, group) + 1)
                        for c in chunks:
                            r, at = rows(which, c), place[which, c]
                            last = nc.tensor.matmul(z_now, w_hi[0:r, at, :],
                                                    product_lo[0:r, part_slot(i, group), c - group.c, :],
                                                    start=False, stop=(ends and c == chunks[-1]))
                    last.then_inc(product_used, 1)

            def dense_1(i):
                pe.wait_ge(logits_ready, i + 1)
                pe.wait_ge(context_loaded, 16 * (i + 1))
                if not is_first(i):
                    pe.wait_ge(y_evac, i)
                parts = [(wt1_10[:, :], logit_10[:, :]), (wt1_2[:, :], logit_2[:, :]),
                         (wt1_ctx[:, :], context_now[:, :])]
                for m in range(HID1 // P):
                    for n, (w, x) in enumerate(parts):
                        last = nc.tensor.matmul(mlp[:, m * P:(m + 1) * P], w[:, m * P:(m + 1) * P], x,
                                                start=(n == 0), stop=(n == len(parts) - 1))
                last.then_inc(h1_ready, 1)

            def dense_2(i):
                pe.wait_ge(h1_evac, i + 1)
                for m in range(HID2 // P):
                    for c in range(HID1 // P):
                        last = nc.tensor.matmul(mlp[:, m * P:(m + 1) * P], wt2[:, c, m * P:(m + 1) * P],
                                                hid1[:, c, :], start=(c == 0), stop=(c == HID1 // P - 1))
                last.then_inc(h2_ready, 1)

            def dense_3(i):
                pe.wait_ge(h2_evac, i + 1)
                for c in range(HID2 // P):
                    last = nc.tensor.matmul(mlp[0:1, 0:P], wt3[:, c:c + 1], hid2[:, c, :],
                                            start=(c == 0), stop=(c == HID2 // P - 1))
                last.then_inc(y_ready, 1)

            pe.wait_ge(ident_loaded, 16)
            turn_block(0)
            pe.wait_ge(w_made, 1)
            contract(None, START[0], 0)
            pe.wait_ge(mlp_w_loaded, 16 * 8)

            def work(i, first=False, last=False):
                for q in range(TILES):
                    tile = TILES * i + q
                    first_layer, next_zeroth, second_layer = layers(i, q, last)
                    contract(i, first_layer, tile)
                    if q == 1 and not first:
                        dense_2(i - 1)
                    if next_zeroth:
                        contract(i, next_zeroth, tile + 1)
                    contract(i, second_layer, tile)
                    if q == 0 and not first:
                        dense_1(i - 1)
                    if q == 1 and not first:
                        dense_3(i - 1)
                    if q == 1 and not last:
                        turn_block(i + 1)

            work(0, first=True)
            with pe.Fori(1, BLOCKS - 1) as i:
                work(i)
            work(BLOCKS - 1, last=True)
            dense_1(BLOCKS - 1)
            dense_2(BLOCKS - 1)
            dense_3(BLOCKS - 1)


def kernel(**inputs):
    import numpy as np
    import concourse.bacc as bacc
    from concourse.bass_utils import run_bass_kernel_spmd

    nc = bacc.Bacc("TRN2", target_bir_lowering=False, num_devices=1)
    arrays, t = {}, {}

    def give(name, a):
        a = np.ascontiguousarray(a)
        arrays["in_" + name] = a
        t[name] = nc.dram_tensor("in_" + name, a.shape, mybir.dt.from_np(a.dtype), kind="ExternalInput").ap()
        return t[name]

    give("ids", inputs["ids"])
    give("ident", np.eye(P, dtype=np.float32))
    give("context_t", np.asarray(inputs["dense_ctx"]).reshape(BLOCKS, P, CONTEXT).transpose(0, 2, 1))
    t["tables"] = [give(f"tbl_{f}", inputs[f"tbl_{f}"]) for f in range(FIELDS)]
    w0 = np.asarray(inputs["L0_rec_w0"])
    give("w0_k_wrapped", np.concatenate([w0, w0], axis=1).reshape(-1, SIZE))
    give("w0_h_wrapped", np.concatenate([w0, w0], axis=0).reshape(-1, SIZE))
    for l in (1, 2):
        give(f"w{l}", np.asarray(inputs[f"L0_rec_w{l}"]).reshape(-1, SIZE))
    for l in range(3):
        give(f"b{l}", inputs[f"L0_rec_b{l}"])
    for name in ("W_top1", "b_top1", "W_top2", "b_top2", "W_top3"):
        give(name, inputs[name])
    t["y"] = nc.dram_tensor("out_y", (BLOCKS, 1, P), mybir.dt.float32, kind="ExternalOutput").ap()
    build(nc, t)
    r = run_bass_kernel_spmd(nc, [arrays], core_ids=[0])
    return np.asarray(r.results[0]["out_y"]).reshape(SAMPLES, 1)
```

```python
from contextlib import ExitStack

import concourse.bass as bass
from concourse import mybir

SAMPLES, FIELDS, DIM = 2048, 39, 16
HALF = 64
SIZE = 128
P = 128
BLOCKS = SAMPLES // P
TILES = 4
D_TILE = DIM // TILES
COLS = D_TILE * P
BLOCK_COLS = TILES * COLS
CHUNKS = (FIELDS * HALF + P - 1) // P
DELTAS = FIELDS // 2 + 1
BANDS = 3
PAIR_CHUNKS = (DELTAS + BANDS - 1) // BANDS
PAIR_ROWS = BANDS * FIELDS
LAST_PAIR_ROWS = (DELTAS - BANDS * (PAIR_CHUNKS - 1)) * FIELDS
WRAPPED = DELTAS - 1 + FIELDS
GROUP = 2
SLOTS = 8
PARTS = 6
PIECE = 4
PIECES = CHUNKS // PIECE
TURN_FIELDS = P // DIM
TURN_PARTS = (FIELDS + TURN_FIELDS - 1) // TURN_FIELDS
TURN_LAST = FIELDS * DIM - (TURN_PARTS - 1) * P
TURNS = 2
TURNED_FIRST = 4 * TURN_FIELDS
AHEAD = (FIELDS + 1) // 2
WHOLE, ON_VECTOR, ON_POOL = "N", "V", "G"
KINDS = {0: "GVNN", 1: "NGVNGNGVNG", 2: "NGVGNGVGNG"}
BEFORE_START = 10
LO_PASSES = 5
LO_LATER = 2
EVAC_AFTER = 3
CONTEXT = 16
HID1, HID2 = 512, 256
GATHERS = (AHEAD, TURNED_FIRST - AHEAD, FIELDS - TURNED_FIRST)
STORES = 16 * 4


def rows(layer, c):
    if layer == 0:
        return LAST_PAIR_ROWS if c == PAIR_CHUNKS - 1 else PAIR_ROWS
    return P


class Group:
    def __init__(self, layer, g, number, split, part):
        chunks = PAIR_CHUNKS if layer == 0 else CHUNKS
        self.layer, self.g, self.c = layer, g, g * GROUP
        self.n = min(GROUP, chunks - self.c)
        self.kind = KINDS[layer][g]
        self.number, self.split, self.part = number, split, part
        assert rows(layer, self.c) == rows(layer, self.c + self.n - 1)


def stretch(layers):
    out, number, split, part = [], 0, 0, {ON_VECTOR: 0, ON_POOL: 0, WHOLE: 0}
    for layer in layers:
        out.append([])
        for g, kind in enumerate(KINDS[layer]):
            out[-1].append(Group(layer, g, number, split, part[kind]))
            number, split = number + 1, split + (kind != WHOLE)
            part[kind] += 1
    for group in (g for layer in out for g in layer):
        group.all = [g for layer in out for g in layer]
        group.splits = [g for layer in out for g in layer if g.kind != WHOLE]
    return out, number, split, part


START, START_GROUPS, START_SPLITS, START_PARTS = stretch([0])
BLOCK, BLOCK_GROUPS, BLOCK_SPLITS, BLOCK_PARTS = stretch([1, 0, 2] * TILES)
assert WHOLE not in (KINDS[1][-1], KINDS[2][-1])
assert BLOCK_GROUPS % SLOTS == 0 and BLOCK_SPLITS % PARTS == 0
LAST, _, _, _ = stretch([1, 0, 2] * (TILES - 1) + [1, 2])


def is_first(i):
    return isinstance(i, int) and i == 0


def number(i, group):
    return group.number if i is None else i * BLOCK_GROUPS + (START_GROUPS + group.number)


def split_number(i, group):
    return group.split if i is None else i * BLOCK_SPLITS + (START_SPLITS + group.split)


def part_number(i, group):
    return group.part if i is None else i * BLOCK_PARTS[group.kind] + (START_PARTS[group.kind] + group.part)


def slot(i, group):
    return (group.number if i is None else START_GROUPS + group.number) % SLOTS


def part_slot(i, group):
    return (group.split if i is None else START_SPLITS + group.split) % PARTS


def slot_before(i, group):
    at = group.number
    while True:
        at -= SLOTS
        if at >= 0:
            where, before = i, group.all[at]
        elif i is None or is_first(i) and -at > START_GROUPS:
            return None, None
        elif is_first(i):
            where, before = None, START[0][at]
        else:
            where, before = i - 1, BLOCK[0][0].all[at]
        if before.kind != ON_VECTOR:
            return where, before


def splits_before(i, group):
    at = group.split - PARTS
    if at >= 0:
        return number(i, group.splits[at])
    if i is None:
        return None
    if is_first(i):
        start = START[0][0].splits
        return number(None, start[at]) if -at <= len(start) else None
    return number(i - 1, BLOCK[0][0].splits[at])


LAYER_GROUPS = {0: START[0], 1: BLOCK[0], 2: BLOCK[2]}


def spare(groups):
    out = []
    for group in groups:
        if group.kind == ON_POOL:
            out.append(-LO_PASSES * group.n)
        if out:
            out[-1] += (4 if group.kind == WHOLE else 3) * group.n
    return [max(0, s) for s in out]


def share(fields, room, n):
    return round(len(fields) * sum(room[:n]) / sum(room))


def layers(i, q, last):
    if last and q == TILES - 1:
        return [LAST[-2], [], LAST[-1]]
    return BLOCK[3 * q:3 * q + 3]


def build(nc, t):
    fp32, fp32r, int32 = mybir.dt.float32, mybir.dt.float32r, mybir.dt.int32
    ALU = mybir.AluOpType
    ACT = mybir.ActivationFunctionType
    AX = mybir.AxisListType

    with ExitStack() as ctx:
        def sb(name, shape, dt=fp32):
            return ctx.enter_context(nc.sbuf_tensor(name, shape, dt))

        def ps(name, shape):
            return ctx.enter_context(nc.psum_tensor(name, shape, fp32))

        def sem(name):
            return ctx.enter_context(nc.semaphore(name))

        x0t_dram = nc.dram_tensor("x0t_scratch", [BLOCKS, WRAPPED, BLOCK_COLS], fp32)

        ids_all = sb("ids_all", [P, BLOCKS, FIELDS], int32)
        ids_now = sb("ids_now", [P, FIELDS], int32)
        gathered_x = sb("gathered_x", [P, FIELDS * DIM])
        x0t = sb("x0t", [P, TURN_PARTS, P])
        ident = sb("ident", [P, P])
        x0_pair = sb("x0_pair", [PAIR_ROWS, PAIR_CHUNKS, COLS])
        x0_stack = sb("x0_stack", [PAIR_ROWS, COLS])
        x0_bcast = sb("x0_bcast", [P, CHUNKS, COLS])
        products = sb("products", [P, SLOTS, GROUP, COLS])
        product_hi = sb("product_hi", [P, PARTS, GROUP, COLS], fp32r)
        product_lo = sb("product_lo", [P, PARTS, GROUP, COLS], fp32r)

        place, whole_chunks, split_chunks = {}, 0, 0
        for layer in range(3):
            for c in range(PAIR_CHUNKS if layer == 0 else CHUNKS):
                if KINDS[layer][c // GROUP] == WHOLE:
                    place[layer, c] = whole_chunks
                    whole_chunks += 1
                else:
                    place[layer, c] = split_chunks
                    split_chunks += 1
        w_whole = sb("w_whole", [P, whole_chunks, SIZE])
        w_hi = sb("w_hi", [P, split_chunks, SIZE], fp32r)
        w_lo = sb("w_lo", [P, split_chunks, SIZE], fp32r)
        staged = x0_bcast[:, :, :].rearrange("p c n -> p (c n)")[:, 0:(2 * PAIR_CHUNKS + 2 * CHUNKS) * SIZE]\
            .rearrange("p (c s) -> p c s", s=SIZE)
        w0_sum, w0_swapped = staged[0:PAIR_ROWS, 0:PAIR_CHUNKS, :], staged[0:PAIR_ROWS, PAIR_CHUNKS:2 * PAIR_CHUNKS, :]
        w1 = staged[:, 2 * PAIR_CHUNKS:2 * PAIR_CHUNKS + CHUNKS, :]
        w2 = staged[:, 2 * PAIR_CHUNKS + CHUNKS:, :]
        arrived = [w0_sum, w1, w2]
        bias = [sb(f"bias{l}", [P, 1]) for l in range(3)]
        direct_10 = sb("direct_10", [P, 2, COLS])
        direct_2 = sb("direct_2", [P, COLS])
        tile_sums_10 = sb("tile_sums_10", [P, TILES, P])
        tile_sums_2 = sb("tile_sums_2", [P, TILES, P])
        logit_10 = sb("logit_10", [P, P])
        logit_2 = sb("logit_2", [P, P])
        context_now = sb("context_now", [CONTEXT, P])
        wt1_10 = sb("wt1_10", [P, HID1])
        wt1_2 = sb("wt1_2", [P, HID1])
        wt1_ctx = sb("wt1_ctx", [CONTEXT, HID1])
        wt2 = sb("wt2", [P, HID1 // P, HID2])
        wt3 = sb("wt3", [P, HID2 // P])
        bt1 = sb("bt1", [P, HID1 // P])
        bt2 = sb("bt2", [P, HID2 // P])
        hid1 = sb("hid1", [P, HID1 // P, P])
        hid2 = sb("hid2", [P, HID2 // P, P])
        y_row = sb("y_row", [1, P])

        z = [ps(f"z_bank{n}", [P, COLS]) for n in range(2)]
        xk = [None, ps("xk1", [P, COLS]), ps("xk2", [P, COLS])]
        x0_stack_now = ps("x0_stack_now", [PAIR_ROWS, COLS])
        split_products = ps("split_products", [P, GROUP, COLS])
        side = ps("side", [P, COLS])

        def z_of(q):
            return z[(q + 1) % 2]

        def product_of(i, group, c, n):
            r, c = rows(group.layer, c), c - group.c
            if group.kind == ON_VECTOR:
                return split_products[0:r, c:c + n, :]
            return products[0:r, slot(i, group), c:c + n, :]

        cin_w_loaded = sem("cin_w_loaded")
        w0_summed = sem("w0_summed")
        w0_diag_loaded = sem("w0_diag_loaded")
        bias_loaded = sem("bias_loaded")
        mlp_w_loaded = sem("mlp_w_loaded")
        ids_loaded = sem("ids_loaded")
        ident_loaded = sem("ident_loaded")
        ids_copied = sem("ids_copied")
        ids_current = sem("ids_current")
        gathered = [sem("gathered_early"), sem("gathered_late"), sem("gathered_last")]
        turned = sem("turned")
        turn_evac = sem("turn_evac")
        x0t_stored = sem("x0t_stored")
        pair_loaded = sem("pair_loaded")
        stack_ready = sem("stack_ready")
        bcast_loaded = [sem(f"bcast_loaded{k}") for k in range(PIECES)]
        context_loaded = sem("context_loaded")
        w_hi_made = sem("w_hi_made")
        w_lo_made = sem("w_lo_made")
        w_made = sem("w_made")
        hi_ready = sem("hi_ready")
        lo_ready = {ON_VECTOR: sem("lo_ready_vector"), ON_POOL: sem("lo_ready_pool")}
        product_ready = sem("product_ready")
        product_used = sem("product_used")
        z_evac = [sem(f"z{l}_evac") for l in range(3)]
        xk_ready = [None, sem("xk1_ready"), sem("xk2_ready")]
        summed_10 = sem("summed_10")
        summed_2 = sem("summed_2")
        logits_ready = sem("logits_ready")
        h1_ready, h1_evac = sem("h1_ready"), sem("h1_evac")
        h2_ready, h2_evac = sem("h2_ready"), sem("h2_evac")
        y_ready, y_evac = sem("y_ready"), sem("y_evac")
        y_stored = sem("y_stored")

        block = ctx.enter_context(nc.Block())

        @block.sync
        def _(sp):
            sp.dma_start(ids_all[:], t["ids"].rearrange("(i p) f -> p i f", p=P)).then_inc(ids_loaded, 16)
            sp.dma_start(ident[:], t["ident"]).then_inc(ident_loaded, 16)

            def store_x0t(i, pairs_used=None):
                sp.wait_ge(turn_evac, TURNS * i + 1)
                rows = x0t_dram[i, :, :].rearrange("f (d b) -> (f d) b", b=P)
                whole = (TURN_PARTS - 1) * P
                again = (WRAPPED - FIELDS) * DIM
                parts = again // P
                for to, n, at in ((0, whole, 0), (whole + TURN_LAST, parts * P, 0),
                                  (whole, TURN_LAST, TURN_PARTS - 1),
                                  (whole + TURN_LAST + parts * P, again - parts * P, parts)):
                    if at == TURN_PARTS - 1:
                        sp.wait_ge(turn_evac, TURNS * (i + 1))
                    if pairs_used is not None and n < P and at < TURN_PARTS - 1:
                        sp.wait_ge(product_ready, pairs_used)
                    if n >= P:
                        to_dram = rows[to:to + n, :].rearrange("(g p) b -> p g b", p=P)
                        sp.dma_start(to_dram, x0t[:, at:at + n // P, :]).then_inc(x0t_stored, 16)
                    else:
                        sp.dma_start(rows[to:to + n, :], x0t[0:n, at, :]).then_inc(x0t_stored, 16)
                sp.wait_ge(x0t_stored, STORES * (i + 1))

            def source(i, row, q, dims):
                at = x0t_dram[i, row, q * COLS:(q + 1) * COLS]
                return bass.AP(at.tensor, at.offset, dims + [[1, COLS]])

            def load_pair(i, q):
                for r in range(BANDS):
                    chunks = len(range(r, DELTAS, BANDS))
                    sp.dma_start(x0_pair[r * FIELDS:(r + 1) * FIELDS, 0:chunks, :],
                                 source(i, r, q, [[BLOCK_COLS, FIELDS], [BANDS * BLOCK_COLS, chunks]]))\
                        .then_inc(pair_loaded, 16)
                    sp.dma_start(x0_stack[r * FIELDS:(r + 1) * FIELDS, :],
                                 source(i, 0, q, [[BLOCK_COLS, FIELDS]])).then_inc(pair_loaded, 16)

            def load_bcast(i, q, k):
                for j in range(2):
                    chunks = len(range(2 * k * PIECE + j, min(FIELDS, 2 * (k + 1) * PIECE), 2))
                    sp.dma_start(x0_bcast[j * HALF:(j + 1) * HALF, k * PIECE:k * PIECE + chunks, :],
                                 source(i, 2 * k * PIECE + j, q, [[0, HALF], [2 * BLOCK_COLS, chunks]]))\
                        .then_inc(bcast_loaded[k], 16)
                if k == PIECES - 1:
                    sp.dma_start(x0_bcast[HALF:P, CHUNKS - 1, :], source(i, FIELDS - 1, q, [[0, HALF]]))\
                        .then_inc(bcast_loaded[k], 16)

            store_x0t(0)
            load_pair(0, 0)
            sp.wait_ge(w_made, 1)
            for k in range(PIECES):
                load_bcast(0, 0, k)
            sp.wait_ge(product_ready, START_GROUPS)
            load_pair(0, 1)

            def loads(i, last=False):
                for q in range(TILES):
                    _, _, second = layers(i, q, last)
                    if q == 2 and not last:
                        store_x0t(i + 1, number(i, second[0]))
                    elif not (last and q >= 2):
                        sp.wait_ge(product_ready, number(i, second[0]))
                    if not (last and q >= 2):
                        load_pair(*((i, q + 2) if q < 2 else (i + 1, q - 2)))
                    if q == 2:
                        if not is_first(i):
                            sp.wait_ge(h1_ready, i)
                        sp.dma_start(context_now[:], t["context_t"][i, :, :]).then_inc(context_loaded, 16)
                    if last and q == TILES - 1:
                        break
                    for k in range(PIECES):
                        sp.wait_ge(product_ready, number(i, second[(k + 1) * PIECE // GROUP - 1]) + 1)
                        load_bcast(*((i, q + 1) if q < TILES - 1 else (i + 1, 0)), k)

            loads(0)
            with sp.Fori(1, BLOCKS - 1) as i:
                loads(i)
            loads(BLOCKS - 1, last=True)

        @block.gpsimd
        def _(pool):
            tables = t["tables"]

            def take_ids(i, late):
                fields = slice(AHEAD, FIELDS) if late else slice(0, AHEAD)
                if not is_first(i):
                    for n in (1, 2) if late else (0,):
                        pool.wait_ge(gathered[n], 16 * GATHERS[n] * i)
                nc.gpsimd.tensor_copy(ids_now[:, fields], ids_all[:, i, fields]).then_inc(ids_copied, 1)
                pool.wait_ge(ids_copied, 2 * i + (2 if late else 1))
                pool.sem_inc(ids_current, 1)

            def gather(f):
                pool.indirect_dma_start(
                    gathered_x[:, f * DIM:(f + 1) * DIM], None, tables[f][:, :],
                    bass.IndirectOffsetOnAxis(ids_now[:, f:f + 1], 0))\
                    .then_inc(gathered[0 if f < AHEAD else 1 if f < TURNED_FIRST else 2], 16)

            def low_part(i, group):
                pool.wait_ge(hi_ready, split_number(i, group) + 1)
                r, at = rows(group.layer, group.c), part_slot(i, group)
                nc.gpsimd.tensor_tensor(product_lo[0:r, at, 0:group.n, :], product_of(i, group, group.c, group.n),
                                        product_hi[0:r, at, 0:group.n, :].bitcast(fp32), ALU.subtract)\
                    .then_inc(lo_ready[ON_POOL], 1)

            pool.wait_ge(ids_loaded, 16)
            for late in (False, True):
                take_ids(0, late)
                for f in range(AHEAD, FIELDS) if late else range(AHEAD):
                    gather(f)
            pool.wait_ge(turned, TURNS)
            take_ids(1, False)
            for f in range(BEFORE_START):
                gather(f)
            for group in START[0]:
                if group.kind == ON_POOL:
                    low_part(None, group)
            for f in range(BEFORE_START, AHEAD):
                gather(f)

            def work(i, next_block, block_after):
                groups = [layers(i, q, not next_block) for q in range(TILES)]
                for part, late in ((groups[:TILES // 2], True), (groups[TILES // 2:], False)):
                    fields = []
                    if late and next_block:
                        take_ids(i + 1, late)
                        pool.wait_ge(turned, TURNS * (i + 1))
                        fields = range(AHEAD, FIELDS)
                    if not late and block_after:
                        pool.wait_ge(turned, TURNS * (i + 1) + 1)
                        take_ids(i + 2, late)
                        fields = range(AHEAD)
                    part = [g for layers_of_tile in part for layer in layers_of_tile for g in layer]
                    room = spare(part)
                    for n, group in enumerate(g for g in part if g.kind == ON_POOL):
                        low_part(i, group)
                        for f in fields[share(fields, room, n):share(fields, room, n + 1)]:
                            gather(f)

            work(0, True, True)
            with pool.Fori(1, BLOCKS - 2) as i:
                work(i, True, True)
            work(BLOCKS - 2, True, False)
            work(BLOCKS - 1, False, False)

        @block.scalar
        def _(act):
            for r in range(BANDS):
                chunks = len(range(r, DELTAS, BANDS))
                part = slice(r * FIELDS, (r + 1) * FIELDS)
                act.dma_start(w0_sum[part, 0:chunks, :],
                              bass.AP(t["w0_k_wrapped"].tensor, r * SIZE,
                                      [[(2 * FIELDS + 1) * SIZE, FIELDS], [BANDS * SIZE, chunks], [1, SIZE]]))\
                    .then_inc(cin_w_loaded, 16)
                act.dma_start(w0_swapped[part, 0:chunks, :],
                              bass.AP(t["w0_h_wrapped"].tensor, r * FIELDS * SIZE,
                                      [[(FIELDS + 1) * SIZE, FIELDS], [BANDS * FIELDS * SIZE, chunks], [1, SIZE]]))\
                    .then_inc(cin_w_loaded, 16)
            whole = (CHUNKS - 1) * P
            for w, name in ((w1, "w1"), (w2, "w2")):
                act.dma_start(w[:, 0:CHUNKS - 1, :], t[name][0:whole, :].rearrange("(c p) s -> p c s", p=P))\
                    .then_inc(cin_w_loaded, 16)
                for j in range(2):
                    act.dma_start(w[j * HALF:(j + 1) * HALF, CHUNKS - 1, :], t[name][whole:, :])\
                        .then_inc(cin_w_loaded, 16)
            for l in range(3):
                act.dma_start(bias[l][:], t[f"b{l}"].rearrange("(p a) -> p a", a=1)).then_inc(bias_loaded, 16)
            act.dma_start(wt1_10[HALF:P, :], t["W_top1"][0:HALF, :]).then_inc(mlp_w_loaded, 16)
            act.dma_start(wt1_10[0:HALF, :], t["W_top1"][HALF:P, :]).then_inc(mlp_w_loaded, 16)
            act.dma_start(wt1_2[:], t["W_top1"][P:2 * P, :]).then_inc(mlp_w_loaded, 16)
            act.dma_start(wt1_ctx[:], t["W_top1"][2 * P:, :]).then_inc(mlp_w_loaded, 16)
            act.dma_start(wt2[:], t["W_top2"].rearrange("(c p) n -> p c n", p=P)).then_inc(mlp_w_loaded, 16)
            with nc.allow_non_contiguous_dma("a few hundred biases and weights, once"):
                act.dma_start(wt3[:], t["W_top3"].rearrange("(c p) a -> p (c a)", p=P)).then_inc(mlp_w_loaded, 16)
                act.dma_start(bt1[:], t["b_top1"].rearrange("(c p) -> p c", p=P)).then_inc(mlp_w_loaded, 16)
                act.dma_start(bt2[:], t["b_top2"].rearrange("(c p) -> p c", p=P)).then_inc(mlp_w_loaded, 16)
            act.wait_ge(w0_summed, 1)
            act.dma_start(w0_sum[0:FIELDS, 0, :],
                          bass.AP(t["w0_h_wrapped"].tensor, 0, [[(FIELDS + 1) * SIZE, FIELDS], [1, SIZE]]))\
                .then_inc(w0_diag_loaded, 16)

            act.wait_ge(w0_diag_loaded, 16)
            for layer in range(3):
                for group in LAYER_GROUPS[layer]:
                    if group.kind != WHOLE:
                        r, at = rows(layer, group.c), place[layer, group.c]
                        last = nc.scalar.copy(w_hi[0:r, at:at + group.n, :],
                                              arrived[layer][0:r, group.c:group.c + group.n, :])
            last.then_inc(w_hi_made, 1)

            def evac_turn(i, half):
                act.wait_ge(turned, TURNS * i + half + 1)
                if half == 0:
                    if not is_first(i):
                        act.wait_ge(x0t_stored, STORES * i)
                    nc.scalar.copy(x0t[:, 0:TURN_PARTS - 1, :], side[:, :].rearrange("p (g b) -> p g b", b=P))\
                        .then_inc(turn_evac, 1)
                else:
                    nc.scalar.copy(x0t[0:TURN_LAST, TURN_PARTS - 1, :], side[0:TURN_LAST, 0:P])\
                        .then_inc(turn_evac, 1)

            def stack(tile):
                act.wait_ge(pair_loaded, 16 * 2 * BANDS * (tile + 1))
                nc.scalar.copy(x0_stack_now[:, :], x0_stack[:]).then_inc(stack_ready, 1)

            def high_part(i, group):
                act.wait_ge(product_ready, number(i, group) + 1)
                before = splits_before(i, group)
                if before is not None:
                    act.wait_ge(product_used, before + 1)
                r, at = rows(group.layer, group.c), part_slot(i, group)
                nc.scalar.copy(product_hi[0:r, at, 0:group.n, :], product_of(i, group, group.c, group.n))\
                    .then_inc(hi_ready, 1)

            def feed(layer, q, contracted):
                act.wait_ge(product_used, contracted)
                for to in range(2):
                    last = nc.scalar.activation(xk[layer + 1][to * HALF:(to + 1) * HALF, :], z_of(q)[0:HALF, :],
                                                ACT.Relu, bias=bias[layer][0:HALF, :])
                last.then_inc(xk_ready[layer + 1], 1)

            def direct_0(i, q, z_now):
                tile = TILES * i + q
                if not (isinstance(tile, int) and tile < 2):
                    act.wait_ge(summed_10, tile - 1)
                nc.scalar.activation(direct_10[HALF:P, q % 2, :], z_now[HALF:P, :], ACT.Relu,
                                     bias=bias[0][HALF:P, :]).then_inc(z_evac[0], 1)

            def direct_1(i, q):
                nc.scalar.activation(direct_10[0:HALF, q % 2, :], z_of(q)[HALF:P, :], ACT.Relu,
                                     bias=bias[1][HALF:P, :]).then_inc(z_evac[1], 1)

            def direct_all(tile, q, contracted):
                act.wait_ge(product_used, contracted)
                if not (isinstance(tile, int) and tile == 0):
                    act.wait_ge(summed_2, tile)
                nc.scalar.activation(direct_2[:, :], z_of(q)[:, :], ACT.Relu, bias=bias[2][:])\
                    .then_inc(z_evac[2], 1)

            def evac_h1(i):
                act.wait_ge(h1_ready, i + 1)
                for m in range(HID1 // P):
                    last = nc.scalar.activation(hid1[:, m, :], side[:, m * P:(m + 1) * P], ACT.Relu,
                                                bias=bt1[:, m:m + 1])
                last.then_inc(h1_evac, 1)

            def evac_h2(i):
                act.wait_ge(h2_ready, i + 1)
                for m in range(HID2 // P):
                    last = nc.scalar.activation(hid2[:, m, :], side[:, m * P:(m + 1) * P], ACT.Relu,
                                                bias=bt2[:, m:m + 1])
                last.then_inc(h2_evac, 1)

            def evac_y(i):
                act.wait_ge(y_ready, i + 1)
                if not is_first(i):
                    act.wait_ge(y_stored, 16 * i)
                nc.scalar.copy(y_row[:], side[0:1, 0:P]).then_inc(y_evac, 1)
                act.wait_ge(y_evac, i + 1)
                act.dma_start(t["y"][i, :, :], y_row[:]).then_inc(y_stored, 16)

            act.wait_ge(bias_loaded, 16 * 3)
            for half in range(TURNS):
                evac_turn(0, half)
            stack(0)
            for group in START[0]:
                if group.kind != WHOLE:
                    high_part(None, group)
            feed(0, 1, START_GROUPS)
            direct_0(0, 0, z_of(1))

            def work(i, first=False, last=False):
                for q in range(TILES):
                    first_layer, next_zeroth, second_layer = layers(i, q, last)

                    tile = TILES * i + q

                    def before_first():
                        if next_zeroth:
                            stack(tile + 1)
                        if not (first and q == 0):
                            direct_all(tile - 1, q - 1, number(i, first_layer[0]))
                        if q == 1 and not first:
                            evac_h2(i - 1)

                    def read_first():
                        feed(1, q, number(i, first_layer[-1]) + 1)
                        direct_1(i, q)
                        if q == 1 and not first:
                            evac_y(i - 1)
                        if q == 2 and not last:
                            evac_turn(i + 1, 1)

                    def before_second():
                        if next_zeroth:
                            feed(0, q + 1, number(i, next_zeroth[-1]) + 1)
                            direct_0(*((i, q + 1) if q < TILES - 1 else (i + 1, 0)), z_of(q + 1))
                        if q == 0 and not first:
                            evac_h1(i - 1)
                        if q == 1 and not last:
                            evac_turn(i + 1, 0)

                    for layer, then in ((first_layer, before_first), (next_zeroth, read_first),
                                        (second_layer, before_second)):
                        if not layer:
                            then()
                        for group in layer:
                            if group.kind != WHOLE:
                                high_part(i, group)
                            if group.g == EVAC_AFTER:
                                then()

            work(0, first=True)
            act.wait_ge(mlp_w_loaded, 16 * 8)
            with act.Fori(1, BLOCKS - 1) as i:
                work(i)
            work(BLOCKS - 1, last=True)
            direct_all(TILES * BLOCKS - 1, TILES - 1, number(BLOCKS - 1, LAST[-1][-1]) + 1)
            evac_h1(BLOCKS - 1)
            evac_h2(BLOCKS - 1)
            evac_y(BLOCKS - 1)
            act.wait_ge(y_stored, 16 * BLOCKS)

        @block.vector
        def _(dve):
            dve.wait_ge(cin_w_loaded, 16 * (2 * BANDS + 2 * 3))
            nc.vector.tensor_add(w0_sum[:, 0:PAIR_CHUNKS - 1, :], w0_sum[:, 0:PAIR_CHUNKS - 1, :],
                                 w0_swapped[:, 0:PAIR_CHUNKS - 1, :])
            nc.vector.tensor_add(w0_sum[0:LAST_PAIR_ROWS, PAIR_CHUNKS - 1, :],
                                 w0_sum[0:LAST_PAIR_ROWS, PAIR_CHUNKS - 1, :],
                                 w0_swapped[0:LAST_PAIR_ROWS, PAIR_CHUNKS - 1, :]).then_inc(w0_summed, 1)
            dve.wait_ge(w0_diag_loaded, 16)
            dve.wait_ge(w_hi_made, 1)
            for layer in range(3):
                for group in LAYER_GROUPS[layer]:
                    c, n = group.c, group.n
                    r, at, w = rows(layer, c), place[layer, c], arrived[layer]
                    if group.kind == WHOLE:
                        nc.vector.tensor_copy(w_whole[0:r, at:at + n, :], w[0:r, c:c + n, :])
                    else:
                        last = nc.vector.tensor_tensor(w_lo[0:r, at:at + n, :], w[0:r, c:c + n, :],
                                                       w_hi[0:r, at:at + n, :].bitcast(fp32), ALU.subtract)
            last.then_inc(w_lo_made, 1)
            dve.wait_ge(w_lo_made, 1)
            for layer in (1, 2):
                at = place[layer, CHUNKS - 1]
                last = nc.vector.tensor_copy(w_hi[HALF:P, at, :], w_lo[HALF:P, at, :])
            last.then_inc(w_made, 1)

            def multiply(i, group):
                at, before = slot_before(i, group)
                if group.kind == ON_VECTOR:
                    if i is not None or group.part > 0:
                        dve.wait_ge(lo_ready[ON_VECTOR], part_number(i, group))
                elif before is not None:
                    if before.kind == WHOLE:
                        dve.wait_ge(product_used, number(at, before) + 1)
                    else:
                        dve.wait_ge(lo_ready[before.kind], part_number(at, before) + 1)
                c, n = group.c, group.n
                r = rows(group.layer, c)
                if group.layer == 0:
                    a, b = x0_stack_now[0:r, :], x0_pair[0:r, c:c + n, :]
                else:
                    a, b = xk[group.layer][0:r, :], x0_bcast[0:r, c:c + n, :]
                nc.vector.tensor_tensor(product_of(i, group, c, n), a.unsqueeze(1).broadcast_to([r, n, COLS]), b,
                                        ALU.mult).then_inc(product_ready, 1)

            def low_part(i, group):
                dve.wait_ge(hi_ready, split_number(i, group) + 1)
                r, at = rows(group.layer, group.c), part_slot(i, group)
                nc.vector.tensor_tensor(product_lo[0:r, at, 0:group.n, :], product_of(i, group, group.c, group.n),
                                        product_hi[0:r, at, 0:group.n, :].bitcast(fp32), ALU.subtract)\
                    .then_inc(lo_ready[ON_VECTOR], 1)

            def make(i, layer, tile=None):
                due = []
                for group in layer:
                    if group.layer == 1 and group.c % PIECE == 0:
                        k = group.c // PIECE
                        dve.wait_ge(bcast_loaded[k], 16 * (3 if k == PIECES - 1 else 2) * (tile + 1))
                    if due and group.kind == ON_VECTOR:
                        low_part(i, due.pop(0))
                    multiply(i, group)
                    if due and due[0].g + LO_LATER <= group.g:
                        low_part(i, due.pop(0))
                    if group.kind == ON_VECTOR:
                        due.append(group)
                for group in due:
                    low_part(i, group)

            def sum_10(i, q):
                dve.wait_ge(z_evac[0], TILES * i + q + 1)
                dve.wait_ge(z_evac[1], TILES * i + q + 1)
                nc.vector.tensor_reduce(tile_sums_10[:, q, :],
                                        direct_10[:, q % 2, :].rearrange("p (d b) -> p b d", b=P),
                                        AX.X, ALU.add).then_inc(summed_10, 1)

            def sum_2(i, q):
                dve.wait_ge(z_evac[2], TILES * i + q + 1)
                nc.vector.tensor_reduce(tile_sums_2[:, q, :], direct_2[:, :].rearrange("p (d b) -> p b d", b=P),
                                        AX.X, ALU.add).then_inc(summed_2, 1)

            def logits(i):
                dve.wait_ge(summed_10, TILES * (i + 1))
                dve.wait_ge(summed_2, TILES * (i + 1))
                if not is_first(i):
                    dve.wait_ge(h1_ready, i)
                for out, sums in ((logit_10, tile_sums_10), (logit_2, tile_sums_2)):
                    last = nc.vector.tensor_reduce(out[:], sums[:, :, :].rearrange("p q b -> p b q"), AX.X, ALU.add)
                last.then_inc(logits_ready, 1)

            dve.wait_ge(pair_loaded, 16 * 2 * BANDS)
            dve.wait_ge(stack_ready, 1)
            make(None, START[0])

            def work(i, first=False, last=False):
                for q in range(TILES):
                    tile = TILES * i + q
                    first_layer, next_zeroth, second_layer = layers(i, q, last)
                    dve.wait_ge(xk_ready[1], tile + 1)
                    make(i, first_layer, tile)
                    if q > 0:
                        sum_2(i, q - 1)
                    elif not first:
                        sum_2(i - 1, TILES - 1)
                        logits(i - 1)
                    if next_zeroth:
                        dve.wait_ge(pair_loaded, 16 * 2 * BANDS * (tile + 2))
                        dve.wait_ge(stack_ready, tile + 2)
                        make(i, next_zeroth)
                    dve.wait_ge(xk_ready[2], tile + 1)
                    make(i, second_layer)
                    if q == 0 and not first:
                        dve.wait_ge(logits_ready, i)
                    sum_10(i, q)

            work(0, first=True)
            with dve.Fori(1, BLOCKS - 1) as i:
                work(i)
            work(BLOCKS - 1, last=True)
            sum_2(BLOCKS - 1, TILES - 1)
            logits(BLOCKS - 1)

        @block.tensor
        def _(pe):
            def turn(i, half):
                if half == 0:
                    for n in range(2):
                        pe.wait_ge(gathered[n], 16 * GATHERS[n] * (i + 1))
                    if not (isinstance(i, int) and i < 2):
                        pe.wait_ge(y_evac, i - 1)
                else:
                    pe.wait_ge(gathered[2], 16 * GATHERS[2] * (i + 1))
                    pe.wait_ge(turn_evac, TURNS * i + 1)
                for g in range(TURN_PARTS - 1) if half == 0 else [TURN_PARTS - 1]:
                    n = TURN_LAST if half else P
                    last = nc.tensor.transpose(side[0:n, g % 4 * P:(g % 4 + 1) * P],
                                               gathered_x[:, g * P:g * P + n], ident[:])
                last.then_inc(turned, 1)

            def contract(i, layer, tile, q):
                which = layer[0].layer
                z_now = z_of(q)[:, :]
                if which == 1:
                    pe.wait_ge(z_evac[0], tile + 1)
                elif which == 2:
                    pe.wait_ge(z_evac[1], tile + 1)
                elif not (isinstance(tile, int) and tile < 2):
                    pe.wait_ge(z_evac[2], tile - 1)
                for group in layer:
                    chunks = range(group.c, group.c + group.n)
                    ends = group is layer[-1]
                    if group.kind == WHOLE:
                        pe.wait_ge(product_ready, number(i, group) + 1)
                        for c in chunks:
                            r = rows(which, c)
                            last = nc.tensor.matmul(z_now, w_whole[0:r, place[which, c], :],
                                                    product_of(i, group, c, 1)[:, 0, :],
                                                    start=(c == 0), stop=(ends and c == chunks[-1]))
                    else:
                        pe.wait_ge(hi_ready, split_number(i, group) + 1)
                        for c in chunks:
                            r, at = rows(which, c), place[which, c]
                            hi = product_hi[0:r, part_slot(i, group), c - group.c, :]
                            nc.tensor.matmul(z_now, w_hi[0:r, at, :], hi, start=(c == 0), stop=False)
                            if which == 0 or c < CHUNKS - 1:
                                nc.tensor.matmul(z_now, w_lo[0:r, at, :], hi, start=False, stop=False)
                        pe.wait_ge(lo_ready[group.kind], part_number(i, group) + 1)
                        for c in chunks:
                            r, at = rows(which, c), place[which, c]
                            if which > 0 and c == CHUNKS - 1:
                                r = HALF
                            last = nc.tensor.matmul(z_now, w_hi[0:r, at, :],
                                                    product_lo[0:r, part_slot(i, group), c - group.c, :],
                                                    start=False, stop=(ends and c == chunks[-1]))
                    last.then_inc(product_used, 1)

            def dense_1(i):
                pe.wait_ge(logits_ready, i + 1)
                pe.wait_ge(context_loaded, 16 * (i + 1))
                parts = [(wt1_10[:, :], logit_10[:, :]), (wt1_2[:, :], logit_2[:, :]),
                         (wt1_ctx[:, :], context_now[:, :])]
                for m in range(HID1 // P):
                    for n, (w, x) in enumerate(parts):
                        last = nc.tensor.matmul(side[:, m * P:(m + 1) * P], w[:, m * P:(m + 1) * P], x,
                                                start=(n == 0), stop=(n == len(parts) - 1))
                last.then_inc(h1_ready, 1)

            def dense_2(i):
                pe.wait_ge(h1_evac, i + 1)
                for m in range(HID2 // P):
                    for c in range(HID1 // P):
                        last = nc.tensor.matmul(side[:, m * P:(m + 1) * P], wt2[:, c, m * P:(m + 1) * P],
                                                hid1[:, c, :], start=(c == 0), stop=(c == HID1 // P - 1))
                last.then_inc(h2_ready, 1)

            def dense_3(i):
                pe.wait_ge(h2_evac, i + 1)
                for c in range(HID2 // P):
                    last = nc.tensor.matmul(side[0:1, 0:P], wt3[:, c:c + 1], hid2[:, c, :],
                                            start=(c == 0), stop=(c == HID2 // P - 1))
                last.then_inc(y_ready, 1)

            pe.wait_ge(ident_loaded, 16)
            for half in range(TURNS):
                turn(0, half)
            pe.wait_ge(w_made, 1)
            contract(None, START[0], 0, 1)

            def work(i, first=False, last=False):
                for q in range(TILES):
                    tile = TILES * i + q
                    first_layer, next_zeroth, second_layer = layers(i, q, last)
                    contract(i, first_layer, tile, q)
                    if q == 1 and not first:
                        dense_3(i - 1)
                    if q == 2 and not last:
                        turn(i + 1, 1)
                    if next_zeroth:
                        contract(i, next_zeroth, tile + 1, q + 1)
                    if q == 0 and not first:
                        dense_1(i - 1)
                    if q == 1 and not last:
                        turn(i + 1, 0)
                    contract(i, second_layer, tile, q)
                    if q == 0 and not first:
                        dense_2(i - 1)

            work(0, first=True)
            pe.wait_ge(mlp_w_loaded, 16 * 8)
            with pe.Fori(1, BLOCKS - 1) as i:
                work(i)
            work(BLOCKS - 1, last=True)
            dense_1(BLOCKS - 1)
            dense_2(BLOCKS - 1)
            dense_3(BLOCKS - 1)


def kernel(**inputs):
    import numpy as np
    import concourse.bacc as bacc
    from concourse.bass_utils import run_bass_kernel_spmd

    nc = bacc.Bacc("TRN2", target_bir_lowering=False, num_devices=1)
    arrays, t = {}, {}

    def give(name, a):
        a = np.ascontiguousarray(a)
        arrays["in_" + name] = a
        t[name] = nc.dram_tensor("in_" + name, a.shape, mybir.dt.from_np(a.dtype), kind="ExternalInput").ap()
        return t[name]

    give("ids", inputs["ids"])
    give("ident", np.eye(P, dtype=np.float32))
    give("context_t", np.asarray(inputs["dense_ctx"]).reshape(BLOCKS, P, CONTEXT).transpose(0, 2, 1))
    t["tables"] = [give(f"tbl_{f}", inputs[f"tbl_{f}"]) for f in range(FIELDS)]
    w0 = np.asarray(inputs["L0_rec_w0"])
    give("w0_k_wrapped", np.concatenate([w0, w0], axis=1).reshape(-1, SIZE))
    give("w0_h_wrapped", np.concatenate([w0, w0], axis=0).reshape(-1, SIZE))
    for l in (1, 2):
        give(f"w{l}", np.asarray(inputs[f"L0_rec_w{l}"]).reshape(-1, SIZE))
    for l in range(3):
        give(f"b{l}", inputs[f"L0_rec_b{l}"])
    for name in ("W_top1", "b_top1", "W_top2", "b_top2", "W_top3"):
        give(name, inputs[name])
    t["y"] = nc.dram_tensor("out_y", (BLOCKS, 1, P), mybir.dt.float32, kind="ExternalOutput").ap()
    build(nc, t)
    r = run_bass_kernel_spmd(nc, [arrays], core_ids=[0])
    return np.asarray(r.results[0]["out_y"]).reshape(SAMPLES, 1)
```
